# Optimizing a Trainium2 kernel written in Bass

```python
import numpy as np
import jax
import jax.numpy as jnp

def _softmax(x, axis=-1):
    return jax.nn.softmax(x, axis=axis)

def _gelu(x):
    return jax.nn.gelu(x, approximate=True)

def _silu(x):
    return jax.nn.silu(x)

def _sigmoid(x):
    return jax.nn.sigmoid(x)

def _layernorm(x, axis=-1, eps=1e-05):
    m = jnp.mean(x, axis=axis, keepdims=True)
    v = jnp.var(x, axis=axis, keepdims=True)
    return (x - m) / jnp.sqrt(v + eps)

def _scatter_add(tgt, idx, src, axis=0):
    return tgt.at[idx].add(src)

def _segment_sum(src, seg, n):
    return jax.ops.segment_sum(src, seg, n)
kernel_name = 'mk_flamingo_gated_d1_seqx_r4_eba8a0'

def setup_inputs(seed: int=0):
    np.random.seed(seed)
    _w = jnp.asarray

    def _rec_inputs():
        import jax
        import jax.numpy as jnp
        _rk = jax.random.key(seed)
        x = -0.0005207 + 1.001 * jax.random.normal(jax.random.fold_in(_rk, 1), (2, 1024, 256), jnp.float32)
        _lenS = 1024 - jax.random.randint(jax.random.fold_in(_rk, 7), (2,), 0, max(1, 1024 // 4) + 1, jnp.int32)
        _lenS2 = 77 - jax.random.randint(jax.random.fold_in(_rk, 8), (2,), 0, max(1, 77 // 4) + 1, jnp.int32)
        _ctx_1024P = jax.random.normal(jax.random.fold_in(_rk, 11), (2, 16, 256), jnp.float32)
        _ctx_1024c = jax.random.dirichlet(jax.random.fold_in(_rk, 511), 0.3 * jnp.ones((16,), jnp.float32), (2, 77))
        _ctx_1024t = jnp.einsum('bsk,bkd->bsd', _ctx_1024c, _ctx_1024P)
        _ctx_1024t = _ctx_1024t * jax.lax.rsqrt(jnp.mean(jnp.square(_ctx_1024t)) + 1e-12) * 0.953939
        ctx_1024 = 4.13588e-05 + 0.999923 * (_ctx_1024t + 0.3 * jax.random.normal(jax.random.fold_in(_rk, 611), (2, 77, 256), jnp.float32))
        _g = jax.random.normal(jax.random.fold_in(_rk, 9001), (2, 1), jnp.float32)
        _g = jnp.sign(_g) * jnp.maximum(jnp.abs(_g), 1.0) + (_g == 0) * 1.0
        g_xattn = _g[0]
        g_ffn = _g[1]
        return (x, ctx_1024, g_xattn, g_ffn)
    x, ctx_1024, g_xattn, g_ffn = _rec_inputs()

    def _L0_xattn_setup():
        import jax, jax.numpy as jnp
        import numpy as np
        D_MODEL = 256
        N_HEADS = 16
        HEAD_DIM = D_MODEL // N_HEADS
        key = jax.random.key(seed)
        ks = jax.random.split(key, 10)
        B, Lq, Lkv = (4, 128, 512)
        s = 1.0 / np.sqrt(D_MODEL)
        return {'q': jax.random.normal(ks[0], (B, Lq, D_MODEL), jnp.float32), 'kv': jax.random.normal(ks[1], (B, Lkv, D_MODEL), jnp.float32), 'Wq': jax.random.normal(ks[2], (D_MODEL, D_MODEL), jnp.float32) * s, 'bq': jnp.zeros((D_MODEL,), jnp.float32), 'Wk': jax.random.normal(ks[3], (D_MODEL, D_MODEL), jnp.float32) * s, 'bk': jnp.zeros((D_MODEL,), jnp.float32), 'Wv': jax.random.normal(ks[4], (D_MODEL, D_MODEL), jnp.float32) * s, 'bv': jnp.zeros((D_MODEL,), jnp.float32), 'Wo': jax.random.normal(ks[5], (D_MODEL, D_MODEL), jnp.float32) * s, 'bo': jnp.zeros((D_MODEL,), jnp.float32)}
    _L0_xattn_all = _L0_xattn_setup()
    _L0_xattn_in = {k: v for k, v in _L0_xattn_all.items() if k in ('Wq', 'bq', 'Wk', 'bk', 'Wv', 'bv', 'Wo', 'bo')}
    del _L0_xattn_all

    def _L0_ffn_setup():
        import jax, jax.numpy as jnp
        import numpy as np
        D, H, E, K = (256, 256, 8, 2)

        def _moe(x, router_w, w_in, b_in, w_out, b_out):
            B, S, Dm = x.shape
            T = B * S
            x2 = x.reshape(T, Dm)
            logits = x2 @ router_w
            probs = jax.nn.softmax(logits, axis=-1)
            top_p, top_e = jax.lax.top_k(probs, K)
            flat_e = top_e.reshape(-1)
            flat_p = top_p.reshape(-1)
            tok = jnp.repeat(jnp.arange(T), K)
            order = jnp.argsort(flat_e)
            se, sp, st = (flat_e[order], flat_p[order], tok[order])
            xd = x2[st]
            N = xd.shape[0]
            h = jnp.zeros((N, H), x.dtype)
            for e in range(E):
                m = (se == e)[:, None]
                h = h + jnp.where(m, jax.nn.gelu(xd @ w_in[e] + b_in[e]), 0.0)
            y = jnp.zeros((N, Dm), x.dtype)
            for e in range(E):
                m = (se == e)[:, None]
                y = y + jnp.where(m, h @ w_out[e] + b_out[e], 0.0)
            y = y * sp[:, None]
            out = jnp.zeros((T, Dm), x.dtype).at[st].add(y)
            return out.reshape(B, S, Dm)
        key = jax.random.key(seed)
        ks = jax.random.split(key, 5)
        s = lambda k, shape, scale: jax.random.normal(k, shape, dtype=jnp.float32) * scale
        return {'input_batch': s(ks[0], (2, 128, D), 1.0), 'router_w': s(ks[1], (D, E), D ** (-0.5)), 'w_in': s(ks[2], (E, D, H), D ** (-0.5)), 'b_in': jnp.zeros((E, H), jnp.float32), 'w_out': s(ks[3], (E, H, D), H ** (-0.5)), 'b_out': jnp.zeros((E, D), jnp.float32)}
    _L0_ffn_all = _L0_ffn_setup()
    _L0_ffn_in = {k: v for k, v in _L0_ffn_all.items() if k in ('router_w', 'w_in', 'b_in', 'w_out', 'b_out')}
    del _L0_ffn_all
    return {'x': x, 'ctx_1024': ctx_1024, 'g_xattn': g_xattn, 'g_ffn': g_ffn, 'L0_xattn_Wq': _L0_xattn_in['Wq'], 'L0_xattn_bq': _L0_xattn_in['bq'], 'L0_xattn_Wk': _L0_xattn_in['Wk'], 'L0_xattn_bk': _L0_xattn_in['bk'], 'L0_xattn_Wv': _L0_xattn_in['Wv'], 'L0_xattn_bv': _L0_xattn_in['bv'], 'L0_xattn_Wo': _L0_xattn_in['Wo'], 'L0_xattn_bo': _L0_xattn_in['bo'], 'L0_ffn_router_w': _L0_ffn_in['router_w'], 'L0_ffn_w_in': _L0_ffn_in['w_in'], 'L0_ffn_b_in': _L0_ffn_in['b_in'], 'L0_ffn_w_out': _L0_ffn_in['w_out'], 'L0_ffn_b_out': _L0_ffn_in['b_out']}

def reference(x, ctx_1024, g_xattn, g_ffn, L0_xattn_Wq, L0_xattn_bq, L0_xattn_Wk, L0_xattn_bk, L0_xattn_Wv, L0_xattn_bv, L0_xattn_Wo, L0_xattn_bo, L0_ffn_router_w, L0_ffn_w_in, L0_ffn_b_in, L0_ffn_w_out, L0_ffn_b_out):
    import jax
    import jax.numpy as jnp

    def _L0_xattn_ref(q, kv, Wq, bq, Wk, bk, Wv, bv, Wo, bo):
        import jax, jax.numpy as jnp
        import numpy as np
        D_MODEL = 256
        N_HEADS = 16
        HEAD_DIM = D_MODEL // N_HEADS
        B, Lq, _ = q.shape
        Lkv = kv.shape[1]
        qh = (q @ Wq.T + bq).reshape(B, Lq, N_HEADS, HEAD_DIM)
        kh = (kv @ Wk.T + bk).reshape(B, Lkv, N_HEADS, HEAD_DIM)
        vh = (kv @ Wv.T + bv).reshape(B, Lkv, N_HEADS, HEAD_DIM)
        scale = 1.0 / np.sqrt(HEAD_DIM).astype(np.float32)
        scores = jnp.einsum('bqhd,bkhd->bhqk', qh, kh) * scale
        attn = jax.nn.softmax(scores, axis=-1)
        ctx = jnp.einsum('bhqk,bkhd->bqhd', attn, vh).reshape(B, Lq, D_MODEL)
        out = ctx @ Wo.T + bo
        return out

    def _L0_ffn_ref(input_batch, router_w, w_in, b_in, w_out, b_out):
        import jax, jax.numpy as jnp
        import numpy as np
        D, H, E, K = (256, 256, 8, 2)

        def _moe(x, router_w, w_in, b_in, w_out, b_out):
            B, S, Dm = x.shape
            T = B * S
            x2 = x.reshape(T, Dm)
            logits = x2 @ router_w
            probs = jax.nn.softmax(logits, axis=-1)
            top_p, top_e = jax.lax.top_k(probs, K)
            flat_e = top_e.reshape(-1)
            flat_p = top_p.reshape(-1)
            tok = jnp.repeat(jnp.arange(T), K)
            order = jnp.argsort(flat_e)
            se, sp, st = (flat_e[order], flat_p[order], tok[order])
            xd = x2[st]
            N = xd.shape[0]
            h = jnp.zeros((N, H), x.dtype)
            for e in range(E):
                m = (se == e)[:, None]
                h = h + jnp.where(m, jax.nn.gelu(xd @ w_in[e] + b_in[e]), 0.0)
            y = jnp.zeros((N, Dm), x.dtype)
            for e in range(E):
                m = (se == e)[:, None]
                y = y + jnp.where(m, h @ w_out[e] + b_out[e], 0.0)
            y = y * sp[:, None]
            out = jnp.zeros((T, Dm), x.dtype).at[st].add(y)
            return out.reshape(B, S, Dm)
        return _moe(input_batch, router_w, w_in, b_in, w_out, b_out)
    x = x + jnp.tanh(g_xattn[0]) * _L0_xattn_ref(_layernorm(x, axis=-1), ctx_1024, L0_xattn_Wq, L0_xattn_bq, L0_xattn_Wk, L0_xattn_bk, L0_xattn_Wv, L0_xattn_bv, L0_xattn_Wo, L0_xattn_bo)
    x = x + jnp.tanh(g_ffn[0]) * _L0_ffn_ref(_layernorm(x, axis=-1), L0_ffn_router_w, L0_ffn_w_in, L0_ffn_b_in, L0_ffn_w_out, L0_ffn_b_out)
    return x

_drawn_inputs = setup_inputs


def setup_inputs(seed=0):
    import zlib

    import numpy as np

    out = dict(_drawn_inputs(seed))
    spreads = {'L0_xattn_bq': (0.0, 0.268),
     'L0_xattn_bk': (0.0, 0.8),
     'L0_xattn_bv': (0.0, 0.1),
     'L0_xattn_bo': (0.0, 0.1),
     'L0_ffn_b_in': (0.0, 0.315),
     'L0_ffn_b_out': (0.0, 0.1)}
    factors = {}
    for name, (base, spread) in spreads.items():
        noise = np.random.default_rng([zlib.crc32(name.encode()), seed]).standard_normal(out[name].shape)
        drawn = base * np.exp(spread * noise) if base else spread * noise
        out[name] = jnp.asarray(drawn.astype(out[name].dtype))
    for name, factor in factors.items():
        out[name] = (out[name] * factor).astype(out[name].dtype)
    return out
```

```python
from contextlib import ExitStack

import numpy as np

import concourse.bass as bass
from concourse import mybir

F32 = mybir.dt.float32
F32R = mybir.dt.float32r
F16 = mybir.dt.float16
I32 = mybir.dt.int32
U32 = mybir.dt.uint32
ALU = mybir.AluOpType
ACT = mybir.ActivationFunctionType
AX_X = mybir.AxisListType.X

P = 128
BATCH, SEQ, D = 2, 1024, 256
KV, NH, DH = 77, 16, 16
E, TOPK = 8, 2
TOK = BATCH * SEQ
TILES = TOK // P
BLK = 4
BLOCKS = TILES // BLK
BN = BLK * P
HH = NH // 2
HALF = HH * KV
CH = 5
CS = HALF // CH
CLEN = [CS] * (CH - 1) + [HALF - CS * (CH - 1)]
VW = DH + 1
PAIRS = TOK * TOPK
NT = (PAIRS - E) // P + E
RING = 4
EPS = 1e-5


def constants():
    p = np.arange(P)
    parts = {
        "ident": np.eye(P),
        "tri": (p[:, None] < p[None, :]),
        "mask_k": (p[:, None] // DH == np.arange(HH)[None, :]),
        "mask_v": np.stack([(CS * k + p)[:, None] // KV == np.arange(HH) for k in range(CH)], 1),
        "iota_p": np.broadcast_to(p, (P, P)),
        "iota_t": np.broadcast_to(np.arange(NT), (P, NT)),
        "iota_e8": np.broadcast_to(np.arange(E) - E, (P, E)),
        "not_first": np.broadcast_to(np.arange(E * TILES) % TILES != 0, (P, E * TILES)),
        "ones_e": np.ones((P, E)),
        "tok1": p[:, None] + P * np.arange(TILES)[None, :] + 1,
        "idle": PAIRS + 1 + p[:, None] + P * np.arange(NT)[None, :],
        "ones_a": np.broadcast_to(((p == 0) | (p == 32))[:, None], (P, P)),
        "ones_b": np.broadcast_to(((p == 64) | (p == 96))[:, None], (P, P)),
        "sel": p[:, None] == (HH * np.arange(2)[:, None] + np.arange(HALF) // KV).reshape(1, -1),
    }
    place, cols, at = {}, [], 0
    for name, a in parts.items():
        a = np.asarray(a, np.float32).reshape(P, -1)
        place[name] = (at, at + a.shape[1])
        at += a.shape[1]
        cols.append(a)
    return np.ascontiguousarray(np.concatenate(cols, 1)), place


def build(nc, a, place):
    ctx = ExitStack()
    with ctx:
        early, late = ExitStack(), ExitStack()

        def sb(name, shape, dt, st=ctx):
            return st.enter_context(nc.sbuf_tensor(name, shape, dt))

        def sem(name):
            return ctx.enter_context(nc.semaphore(name))

        n_small = place["sel"][0]
        x_sb = sb("x_sb", [P, TILES, D], F32)
        cst = sb("cst", [P, n_small], F32)
        gates_in = sb("gates_in", [P, 2], F32)
        tg = sb("tg", [P, 2], F32)
        w_hi = [sb(f"w{n}_hi", [P, E * 2 * D], F32R) for n in ("in", "out")]
        w_lo = [sb(f"w{n}_lo", [P, E * 2 * D], F32R) for n in ("in", "out")]
        btab = sb("btab", [P, E * D], F32R)
        ones_a = sb("ones_a", [P, P], F32R)
        ones_b = sb("ones_b", [P, P], F32R)
        tri16 = sb("tri16", [P, 2, P], F16)
        lg = sb("lg", [P, TILES, E], F32)

        wq_hi = sb("wq_hi", [P, 2, D], F32R, early)
        wq_lo = sb("wq_lo", [P, 2, D], F32R, early)
        kb_hi = sb("kb_hi", [P, BATCH, 2, HALF], F32R, early)
        kb_lo = sb("kb_lo", [P, BATCH, 2, HALF], F32R, early)
        sel = sb("sel", [P, 2, HALF], F32R, early)
        qT_hi = sb("qT_hi", [P, 3, BN], F32R, early)
        qT_lo = sb("qT_lo", [P, 3, BN], F32R, early)
        z_sb = sb("z_sb", [P, BLK, D], F32, early)
        zT_hi = sb("zT_hi", [P, 2, BN], F32R, early)
        zT_lo = sb("zT_lo", [P, 2, BN], F32R, early)
        vb = sb("vb", [P, BATCH, 2, CH, HH * VW], F32, early)
        prob = sb("prob", [P, 2 * CH * BN], F32, early)
        m_sb = sb("m_sb", [P, 2, BN], F32R, early)
        c_sb = sb("c_sb", [P, BLK, D], F32, early)
        wo_hi = sb("wo_hi", [P, 2, D], F32R, early)
        wo_lo = sb("wo_lo", [P, 2, D], F32R, early)
        obias = sb("obias", [P, D], F32R, early)
        stage = sb("stage", [P, 2, 2 * D], F32, early)
        kT = sb("kT", [P, 2, 2 * KV], F32, early)
        kT_hi = sb("kT_hi", [P, 2, 2 * KV], F32, early)
        kT_lo = sb("kT_lo", [P, 2, 2 * KV], F32, early)
        bcol = sb("bcol", [P, 6], F32, early)
        brow = sb("brow", [1, 2, D], F32, early)
        mx = sb("mx", [P, BLK, NH], F32, early)
        st6 = sb("st6", [P, 2, BLK, 6], F32, early)
        mv = sb("mv", [P, 2, BLK, 2], F32, early)
        rstd = sb("rstd", [P, 2, BLK], F32, early)
        veps = sb("veps", [P, 2, BLK], F32, early)
        half = sb("half", [P, BLK], F32, early)
        rden = sb("rden", [P, BLK, HH], F32, early)
        z2T = sb("z2T", [P, 2, BN], F32, early)
        rw = sb("rw", [P, 2, E], F32, early)
        z2_sb = sb("z2_sb", [P, BLK, D], F32, early)
        at = [0]

        def setup_view(n):
            at[0] += n
            return prob[:, at[0] - n:at[0]]

        ctxT = setup_view(2 * 2 * KV).rearrange("p (k n) -> p k n", k=2)
        ctx_rep = setup_view(2 * 2 * HALF).rearrange("p (k b n) -> p k b n", k=2, b=2)
        wk_sb = setup_view(2 * D).rearrange("p (k n) -> p k n", k=2)
        wv_sb = setup_view(2 * D).rearrange("p (k n) -> p k n", k=2)
        sel_f = setup_view(2 * HALF)
        early.close()

        def mo(name, shape, dt):
            return sb(name, shape, dt, late)

        pr = mo("pr", [P, TILES, E], F32)
        tmp = mo("tmp", [P, TILES, E], F32)
        m1 = mo("m1", [P, TILES, E], F32)
        m2 = mo("m2", [P, TILES, E], F32)
        m16 = mo("m16", [P, TILES, E], F16)
        red1 = mo("red1", [P, TILES], F32)
        red2 = mo("red2", [P, TILES], F32)
        ptop = mo("ptop", [P, TOPK, TILES], F32)
        cnt = mo("cnt", [P, E, TILES], F32)
        inc = mo("inc", [P, E, TILES], F32)
        base = mo("base", [P, E, TILES], F32)
        pos3 = mo("pos3", [P, TILES, E], F32)
        seli = mo("seli", [P, TOPK, TILES, E], F32)
        pos = mo("pos", [P, TOPK * TILES], F32)
        pos_i = mo("pos_i", [P, TOPK * TILES], I32)
        pa_i = mo("pa_i", [P, TOPK * TILES], I32)
        pb_i = mo("pb_i", [P, TOPK * TILES], I32)
        pa = mo("pa", [P, TOPK * TILES], F32)
        pb = mo("pb", [P, TOPK * TILES], F32)
        nt_i = mo("nt_i", [P, E], I32)
        nt_s = mo("nt_s", [P, E], I32)
        nt = mo("nt", [P, E], F32)
        ends = mo("ends", [P, E], F32)
        starts = mo("starts", [P, E], F32)
        le = mo("le", [1, NT, E], F32)
        ex_f = mo("ex_f", [1, NT], F32)
        ex_i = mo("ex_i", [1, NT], I32)
        hot_b = mo("hot_b", [P, TOPK * TILES, P], F16)
        hot_a = mo("hot_a", [P, TOPK * TILES, NT], F32)
        val_a = mo("val_a", [P, TOPK * TILES, NT], F16)
        tab = mo("tab", [P, 5, NT], F32)
        src_i = mo("src_i", [P, NT], U32)
        dst_i = mo("dst_i", [P, NT], U32)
        xg = mo("xg", [P, RING, D], F32)
        xT_hi = mo("xT_hi", [P, 2, D], F32R)
        xT_lo = mo("xT_lo", [P, 2, D], F32R)
        h_sb = mo("h_sb", [P, 2, D], F32)
        hT_hi = mo("hT_hi", [P, 2, D], F32R)
        hT_lo = mo("hT_lo", [P, 2, D], F32R)
        y_sb = mo("y_sb", [P, RING, D], F32)
        yc = [mo(f"yc{k}", [P, TILES, D], F32) for k in range(TOPK)]
        late.close()

        def pair(name):
            return ctx.enter_context(nc.psum_tensor(name, [P, 2, 512], F32))

        pG = pair("pG")
        pM = pair("pM")
        pS = pair("pS")
        pV = pair("pV")

        z_dram = nc.dram_tensor("z_dram", [TOK, D], F32, kind="Internal").ap()
        y_dram = nc.dram_tensor("y_dram", [PAIRS + NT * P, D], F32, kind="Internal").ap()

        s_x = [sem(f"s_x{b}") for b in range(BLOCKS)]
        s_ctx, s_wkv, s_cst, s_sel = sem("s_ctx"), sem("s_wkv"), sem("s_cst"), sem("s_sel")
        s_wq, s_wo, s_bias, s_brow, s_rw = sem("s_wq"), sem("s_wo"), sem("s_bias"), sem("s_brow"), sem("s_rw")
        s_stage = [sem("s_stage0"), sem("s_stage1")]
        s_bst = [sem("s_bst0"), sem("s_bst1")]
        s_zd = [sem("s_zd0"), sem("s_zd1")]
        s_xg = [sem(f"s_xg{r}") for r in range(RING)]
        s_ys = [sem(f"s_ys{r}") for r in range(RING)]
        s_yc = [sem(f"s_yc{b}") for b in range(BLOCKS)]
        s_out = sem("s_out")
        dve_step, pool_step, act_step = sem("dve_step"), sem("pool_step"), sem("act_step")
        rep_ready, wq_h, wo_h, tg_ready = sem("rep_ready"), sem("wq_h"), sem("wo_h"), sem("tg_ready")
        wq_ready, wo_ready = sem("wq_ready"), sem("wo_ready")
        k_ps, kt_ready, kb_ready, v_ps, v_ready = sem("k_ps"), sem("kt_ready"), sem("kb_ready"), sem("v_ps"), sem("v_ready")
        bo_ps, ob_ready, cst_ready, m_zero = sem("bo_ps"), sem("ob_ready"), sem("cst_ready"), sem("m_zero")
        bst_zero, bst_used, btab_ready, stage_used = sem("bst_zero"), sem("bst_used"), sem("btab_ready"), sem("stage_used")
        var1, var2, rstd1, rstd2 = sem("var1"), sem("var2"), sem("rstd1"), sem("rstd2")
        z_ready, zT_ps, z_hi, z_lo = sem("z_ready"), sem("zT_ps"), sem("z_hi"), sem("z_lo")
        q_ps, q_hi, q_lo = sem("q_ps"), sem("q_hi"), sem("q_lo")
        sm_ps, sm_red, mT_ps, m_ready = sem("sm_ps"), sem("sm_red"), sem("mT_ps"), sem("m_ready")
        s_ps, exp_done, pv_ps, normed = sem("s_ps"), sem("exp_done"), sem("pv_ps"), sem("normed")
        cT_ps, c_hi, c_lo, o_ps = sem("cT_ps"), sem("c_hi"), sem("c_lo"), sem("o_ps")
        x1_ready, z2_ready, z2T_ps, z2T_ready = sem("x1_ready"), sem("z2_ready"), sem("z2T_ps"), sem("z2T_ready")
        lg_ps, lg_ready = sem("lg_ps"), sem("lg_ready")
        dif_ready, e_ready, m_done, rank_ps = sem("dif_ready"), sem("e_ready"), sem("m_done"), sem("rank_ps")
        hot_ready, tab_ps, ex_ready, idx_ready = sem("hot_ready"), sem("tab_ps"), sem("ex_ready"), sem("idx_ready")
        xT_ps, x_hi, x_lo = sem("xT_ps"), sem("x_hi"), sem("x_lo")
        h_ps, h_ready, hT_ps, h_hi, h_lo = sem("h_ps"), sem("h_ready"), sem("hT_ps"), sem("h_hi"), sem("h_lo")
        y_ps, y_ready, out_ready = sem("y_ps"), sem("y_ready"), sem("out_ready")

        def c(name):
            lo, hi = place[name]
            return cst[:, lo:hi]

        ident = c("ident")
        x_t = a["x"].rearrange("(b t p) d -> b p t d", p=P, t=BLK)
        out_t = a["out"].rearrange("(b t p) d -> b p t d", p=P, t=BLK)
        z_t = z_dram.rearrange("(b t p) d -> b p t d", p=P, t=BLK)
        y_t = y_dram[0:PAIRS, :].rearrange("(k b t p) d -> k b p t d", p=P, t=BLK, k=TOPK)

        def unit(blk, half):
            return (2 * blk + half) % 3

        block = ctx.enter_context(nc.Block())

        @block.sync
        def _(sp):
            def two(w):
                return w.rearrange("(k p) n -> p k n", p=P)

            sp.dma_start(x_sb[:, 0:BLK, :], x_t[0]).then_inc(s_x[0], 16)
            sp.dma_start(ctxT, two(a["ctx_t"])).then_inc(s_ctx, 16)
            sp.dma_start(wk_sb, two(a["wk_t"])).then_inc(s_wkv, 16)
            sp.dma_start(cst[:], a["const"][:, 0:n_small]).then_inc(s_cst, 16)
            sp.dma_start(bcol[:], a["bcol"]).then_inc(s_bias, 16)
            sp.dma_start(stage[:, 0, :].rearrange("p (k n) -> p k n", k=2), two(a["wq_t"])).then_inc(s_wq, 16)
            sp.dma_start(wv_sb, two(a["wv_t"])).then_inc(s_wkv, 16)
            sp.dma_start(sel_f, a["const"][:, n_small:]).then_inc(s_sel, 16)
            sp.dma_start(stage[:, 1, :].rearrange("p (k n) -> p k n", k=2), two(a["wo_t"])).then_inc(s_wo, 16)
            sp.dma_start(brow[0:1, 0, :], a["bo"]).then_inc(s_brow, 16)
            sp.dma_start(gates_in[:], a["gates"]).then_inc(s_brow, 16)
            sp.dma_start(x_sb[:, BLK:2 * BLK, :], x_t[1]).then_inc(s_x[1], 16)
            sp.dma_start(rw[:], a["router"].rearrange("(k p) e -> p k e", p=P)).then_inc(s_rw, 16)
            for b in range(2, BLOCKS):
                sp.dma_start(x_sb[:, b * BLK:(b + 1) * BLK, :], x_t[b]).then_inc(s_x[b], 16)
            for g in range(2):
                sp.wait_ge(bst_zero, 1)
                if g:
                    sp.wait_ge(bst_used, 1)
                for row, name in ((0, "b_in"), (32, "b_in"), (64, "b_out"), (96, "b_out")):
                    sp.dma_start(z2_sb[row:row + 1, :, :].rearrange("p e d -> p (e d)"),
                                 a[name][:, g * BLK * D:(g + 1) * BLK * D]).then_inc(s_bst[g], 16)
            sp.wait_ge(wq_ready, 1)
            for u in range(2 * E):
                e, which = u // 2, u % 2
                if u == 1:
                    sp.wait_ge(wo_ready, 1)
                    sp.wait_ge(bo_ps, 1)
                if u >= 2:
                    sp.wait_ge(stage_used, u - 1)
                w = a["w_out" if which else "w_in"]
                sp.dma_start(stage[:, u % 2, :].rearrange("p (k n) -> p k n", k=2),
                             w[e].rearrange("(k p) n -> p k n", p=P)).then_inc(s_stage[u % 2], 16)
            for b in range(BLOCKS):
                sp.wait_ge(z2_ready, b + 1)
                sp.dma_start(z_t[b], z2_sb[:]).then_inc(s_zd[b % 2], 16)
            for r in range(RING):
                sp.wait_ge(s_ys[r], 16 * len(range(r, NT, RING)))
            for b in range(BLOCKS):
                for k in range(TOPK):
                    sp.dma_start(yc[k][:, b * BLK:(b + 1) * BLK, :], y_t[k, b]).then_inc(s_yc[b], 16)
            for b in range(BLOCKS):
                sp.wait_ge(out_ready, b + 1)
                sp.dma_start(out_t[b], x_sb[:, b * BLK:(b + 1) * BLK, :]).then_inc(s_out, 16)
            sp.wait_ge(s_out, 16 * BLOCKS)

        @block.gpsimd
        def _(pool):
            step = [0]

            def link(ins):
                step[0] += 1
                ins.then_inc(pool_step, 1)
                pool.wait_ge(pool_step, step[0])

            def inv_std(which, n, src, done):
                pool.wait_ge(src, n + 1)
                link(nc.gpsimd.tensor_scalar(veps[:, which, :], mv[:, which, :, 1], EPS, None, ALU.add))
                nc.gpsimd.tensor_tensor(rstd[:, which, :], veps[:, which, :], half[:],
                                        ALU.pow).then_inc(done, 1)

            def split_weights(u0, u1):
                for u in range(u0, u1):
                    e, which = u // 2, u % 2
                    sl = slice(e * 2 * D, (e + 1) * 2 * D)
                    pool.wait_ge(s_stage[u % 2], 16 * (u // 2 + 1))
                    link(nc.gpsimd.tensor_copy(w_hi[which][:, sl], stage[:, u % 2, :]))
                    nc.gpsimd.tensor_tensor(w_lo[which][:, sl], stage[:, u % 2, :],
                                            w_hi[which][:, sl].bitcast(F32),
                                            ALU.subtract).then_inc(stage_used, 1)

            nc.gpsimd.memset(z2_sb[:], 0.0).then_inc(bst_zero, 1)
            link(nc.gpsimd.memset(half[:], -0.5))
            nc.gpsimd.memset(obias[:].bitcast(F32), 0.0).then_inc(m_zero, 1)
            nc.gpsimd.memset(m_sb[:].bitcast(F32), 0.0).then_inc(m_zero, 1)
            inv_std(0, 0, var1, rstd1)
            for g in range(2):
                pool.wait_ge(s_bst[g], 64)
                sl = slice(g * BLK * D, (g + 1) * BLK * D)
                src = z2_sb[:].rearrange("p e d -> p (e d)")
                link(nc.gpsimd.tensor_copy(btab[:, sl], src))
                for row in (32, 96):
                    last = nc.gpsimd.tensor_tensor(btab[row:row + 1, sl], src[row:row + 1, :],
                                                   btab[row:row + 1, sl].bitcast(F32), ALU.subtract)
                    if row == 32:
                        link(last)
                last.then_inc(bst_used, 1)
                pool.wait_ge(bst_used, g + 1)
                if g == 0:
                    inv_std(0, 1, var1, rstd1)
            for b in range(BLOCKS):
                split_weights(4 * b, 4 * b + 4)
                if b >= 1:
                    inv_std(1, b - 1, var2, rstd2)
                if b + 2 < BLOCKS:
                    inv_std(0, b + 2, var1, rstd1)
            inv_std(1, BLOCKS - 1, var2, rstd2)

            def gather(j):
                r = j % RING
                if j >= RING:
                    pool.wait_ge(xT_ps, j - RING + 1)
                pool.indirect_dma_start(
                    out=xg[:, r, :], out_offset=None, in_=z_dram,
                    in_offset=bass.IndirectOffsetOnAxis(ap=src_i[:, j:j + 1], axis=0),
                ).then_inc(s_xg[r], 16)

            def scatter(j):
                r = j % RING
                pool.wait_ge(y_ready, j + 1)
                pool.indirect_dma_start(
                    out=y_dram, out_offset=bass.IndirectOffsetOnAxis(ap=dst_i[:, j:j + 1], axis=0),
                    in_=y_sb[:, r, :], in_offset=None,
                ).then_inc(s_ys[r], 16)

            for b in range(2):
                pool.wait_ge(s_zd[b], 16 * (BLOCKS // 2))
            pool.wait_ge(idx_ready, 1)
            for j in range(RING):
                gather(j)
            for j in range(NT):
                scatter(j)
                if j + RING < NT:
                    gather(j + RING)

        @block.scalar
        def _(act):
            act.wait_ge(s_ctx, 16)
            for k in range(2):
                for b in range(BATCH):
                    last = nc.scalar.activation(
                        ctx_rep[:, k, b, :].rearrange("p (h n) -> p h n", h=HH),
                        ctxT[:, k, b * KV:(b + 1) * KV].unsqueeze(1).broadcast_to([P, HH, KV]), ACT.Copy)
            last.then_inc(rep_ready, 1)
            act.wait_ge(s_wq, 16)
            nc.scalar.activation(wq_hi[:].rearrange("p k n -> p (k n)"), stage[:, 0, :], ACT.Copy).then_inc(wq_h, 1)
            act.wait_ge(s_brow, 32)
            nc.scalar.activation(tg[:], gates_in[:], ACT.Tanh).then_inc(tg_ready, 1)

            def split_z(b):
                act.wait_ge(zT_ps, b + 1)
                if b >= 3:
                    act.wait_ge(o_ps, b - 2)
                nc.scalar.activation(zT_hi[:], pG[:], ACT.Copy).then_inc(z_hi, 1)

            def split_q(b, h):
                act.wait_ge(q_ps, 2 * b + h + 1)
                if 2 * b + h >= 3:
                    act.wait_ge(s_ps, CH * (2 * b + h - 2))
                nc.scalar.activation(qT_hi[:, unit(b, h), :], pG[:, h, :], ACT.Identity,
                                     bias=bcol[:, h:h + 1]).then_inc(q_hi, 1)

            def negate_max(b):
                act.wait_ge(mT_ps, b + 1)
                if b >= 2:
                    act.wait_ge(s_ps, 2 * CH * (b - 1))
                nc.scalar.activation(m_sb[0:NH, b % 2, :], pM[0:NH, 0, :], ACT.Copy,
                                     scale=-1.0).then_inc(m_ready, 1)

            def exp(b, s):
                h, k = s // CH, s % CH
                n = 2 * CH * b + s
                act.wait_ge(s_ps, n + 1)
                if b >= 1 and k == 0:
                    act.wait_ge(pv_ps, BLK * (2 * (b - 1) + h + 1))
                nc.scalar.activation(prob[0:CLEN[k], s * BN:(s + 1) * BN], pS[0:CLEN[k], n % 2, :],
                                     ACT.Exp).then_inc(exp_done, 1)

            def split_c(b):
                act.wait_ge(cT_ps, b + 1)
                act.wait_ge(q_ps, min(2 * (b + 3), 2 * BLOCKS))
                nc.scalar.activation(zT_hi[:], pG[:], ACT.Copy).then_inc(c_hi, 1)

            def copy_z2(b):
                act.wait_ge(z2T_ps, b + 1)
                if b >= 1:
                    act.wait_ge(lg_ps, b)
                nc.scalar.activation(z2T[:], pG[:], ACT.Copy).then_inc(z2T_ready, 1)

            act.wait_ge(s_bias, 16)
            for b in range(-1, BLOCKS + 2):
                main = 0 <= b < BLOCKS
                nxt = b + 1 < BLOCKS
                prev = 1 <= b <= BLOCKS
                for s in range(2 * CH):
                    if main:
                        if b == 0 and s == 0:
                            act.wait_ge(v_ps, BATCH * CH)
                            act.wait_ge(cst_ready, 1)
                        exp(b, s)
                    if s == 0 and b >= 2:
                        copy_z2(b - 2)
                    if s == 1 and nxt:
                        split_z(b + 1)
                    if s == 0 and b == -1:
                        act.wait_ge(s_wo, 16)
                        nc.scalar.activation(wo_hi[:].rearrange("p k n -> p (k n)"), stage[:, 1, :],
                                             ACT.Copy).then_inc(wo_h, 1)
                    if s == 2 and nxt:
                        split_q(b + 1, 0)
                    if s == 5 and nxt:
                        split_q(b + 1, 1)
                    if s == 6 and prev:
                        split_c(b - 1)
                if nxt:
                    if b == -1:
                        act.wait_ge(m_zero, 2)
                    negate_max(b + 1)

            act.wait_ge(dif_ready, 1)
            nc.scalar.activation(tmp[:], pr[:], ACT.Exp).then_inc(e_ready, 1)

            def x_high(j):
                act.wait_ge(xT_ps, j + 1)
                if j >= 2:
                    act.wait_ge(h_ps, j - 1)
                nc.scalar.activation(xT_hi[:, j % 2, :], pG[:, j % 2, 0:D], ACT.Copy).then_inc(x_hi, 1)

            def gelu(j):
                act.wait_ge(h_ps, j + 1)
                if j >= 2:
                    act.wait_ge(hT_ps, j - 1)
                nc.scalar.activation(h_sb[:, j % 2, :], pM[:, j % 2, 0:D],
                                     ACT.Gelu_apprx_tanh).then_inc(h_ready, 1)

            def h_high(j):
                act.wait_ge(hT_ps, j + 1)
                if j >= 2:
                    act.wait_ge(y_ps, j - 1)
                nc.scalar.activation(hT_hi[:, j % 2, :], pS[:, j % 2, 0:D], ACT.Copy).then_inc(h_hi, 1)

            x_high(0)
            for j in range(NT + 1):
                if j >= 1:
                    h_high(j - 1)
                if j + 1 < NT:
                    x_high(j + 1)
                if j < NT:
                    gelu(j)

        @block.vector
        def _(dve):
            step = [0]

            def link(ins):
                step[0] += 1
                ins.then_inc(dve_step, 1)
                dve.wait_ge(dve_step, step[0])

            def stats(which, src, done):
                for i in range(BLK):
                    last = nc.vector.bn_stats(st6[:, which, i, :], src[:, i, :])
                link(last)
                for i in range(BLK):
                    last = nc.vector.bn_aggr(mv[:, which, i, :], st6[:, which, i, :])
                last.then_inc(done, 1)

            def normalise(which, n, src, dst, inv, done):
                dve.wait_ge(inv, n + 1)
                for i in range(BLK):
                    last = nc.vector.tensor_scalar(dst[:, i, :], src[:, i, :], mv[:, which, i, 0:1],
                                                   rstd[:, which, i:i + 1], ALU.subtract, ALU.mult)
                last.then_inc(done, 1)

            def xs(b):
                return x_sb[:, b * BLK:(b + 1) * BLK, :]

            def norm1(b):
                if b >= 1:
                    dve.wait_ge(zT_ps, b)
                normalise(0, b, xs(b), z_sb, rstd1, z_ready)

            def split_z(b):
                dve.wait_ge(z_hi, b + 1)
                nc.vector.tensor_tensor(zT_lo[:], pG[:], zT_hi[:].bitcast(F32), ALU.subtract).then_inc(z_lo, 1)

            def split_q(b, h):
                dve.wait_ge(q_hi, 2 * b + h + 1)
                u = unit(b, h)
                nc.vector.scalar_tensor_tensor(out=qT_lo[:, u, :], in0=pG[:, h, :], scalar=bcol[:, h:h + 1],
                                               in1=qT_hi[:, u, :].bitcast(F32), op0=ALU.add,
                                               op1=ALU.subtract).then_inc(q_lo, 1)

            def reduce_max(b, h, i):
                n = 8 * b + 4 * h + i
                dve.wait_ge(sm_ps, n + 1)
                if b >= 1 and n % 8 == 0:
                    dve.wait_ge(mT_ps, b)
                nc.vector.tensor_reduce(mx[:, i, h * HH:(h + 1) * HH].rearrange("p (a h) -> p a h", a=2),
                                        pM[:, :, 0:4 * KV].rearrange("p a (h n) -> p a h n", n=KV),
                                        AX_X, ALU.max).then_inc(sm_red, 1)

            def normalise_attention(b, h):
                n = 2 * b + h
                dve.wait_ge(pv_ps, BLK * (n + 1))
                v = pV[:].rearrange("p a (t w) -> p (a t) w", t=2)[:, :, 0:HH * VW].rearrange(
                    "p t (h w) -> p t h w", w=VW)
                link(nc.vector.reciprocal(rden[:], v[:, :, :, DH]))
                if b >= 1 and h == 0:
                    dve.wait_ge(cT_ps, b)
                nc.vector.tensor_tensor(
                    c_sb[:, :, h * P:(h + 1) * P].rearrange("p t (h w) -> p t h w", w=DH),
                    v[:, :, :, 0:DH], rden[:].unsqueeze(3).broadcast_to([P, BLK, HH, DH]),
                    ALU.mult).then_inc(normed, 1)

            def split_c(b):
                dve.wait_ge(c_hi, b + 1)
                nc.vector.tensor_tensor(zT_lo[:], pG[:], zT_hi[:].bitcast(F32), ALU.subtract).then_inc(c_lo, 1)

            def residual(b):
                if b == 0:
                    dve.wait_ge(tg_ready, 1)
                dve.wait_ge(o_ps, b + 1)
                dve.wait_ge(z_ready, b + 1)
                x4 = xs(b).rearrange("p (a t) d -> p a (t d)", a=2)
                step[0] += 1
                nc.vector.scalar_tensor_tensor(out=x4, in0=pG[:], scalar=tg[:, 0:1], in1=x4,
                                               op0=ALU.mult, op1=ALU.add).then_inc(dve_step, 1)
                dve.wait_ge(dve_step, step[0])
                dve.wait_ge(rstd2, b) if b else None
                stats(1, xs(b), var2)

            def norm2(b):
                if b >= 1:
                    dve.wait_ge(s_zd[(b - 1) % 2], 16 * ((b - 1) // 2 + 1))
                    dve.wait_ge(z2T_ps, b)
                else:
                    dve.wait_ge(bst_used, 2)
                normalise(1, b, xs(b), z2_sb, rstd2, z2_ready)

            def take_logits(b):
                dve.wait_ge(lg_ps, b + 1)
                nc.vector.tensor_copy(lg[:, b * BLK:(b + 1) * BLK, :].rearrange("p t e -> p (t e)"),
                                      pM[:, 0, 0:BLK * E]).then_inc(lg_ready, 1)

            dve.wait_ge(s_x[0], 16)
            stats(0, xs(0), var1)
            dve.wait_ge(wq_h, 1)
            nc.vector.tensor_tensor(wq_lo[:].rearrange("p k n -> p (k n)"), stage[:, 0, :],
                                    wq_hi[:].rearrange("p k n -> p (k n)").bitcast(F32),
                                    ALU.subtract).then_inc(wq_ready, 1)
            norm1(0)
            dve.wait_ge(s_bias, 16)
            for h in range(2):
                dve.wait_ge(k_ps, h + 1)
                last = nc.vector.tensor_scalar(kT[:, h, :], pS[:, h, 0:2 * KV], bcol[:, 2 + h:3 + h],
                                               DH ** -0.5, ALU.add, ALU.mult)
            link(last)
            link(nc.vector.tensor_copy(kT_hi[:].bitcast(F32R), kT[:]))
            link(nc.vector.tensor_tensor(kT_lo[:], kT[:], kT_hi[:], ALU.subtract))
            dve.wait_ge(s_cst, 16)
            split_z(0)
            for b in range(BATCH):
                for part, dst in ((kT_hi, kb_hi), (kT_lo, kb_lo)):
                    for h in range(2):
                        nc.vector.tensor_tensor(
                            dst[:, b, h, :].rearrange("p (h n) -> p h n", n=KV),
                            part[:, h, b * KV:(b + 1) * KV].unsqueeze(1).broadcast_to([P, HH, KV]),
                            c("mask_k").unsqueeze(2).broadcast_to([P, HH, KV]),
                            ALU.mult).then_inc(kb_ready, 1)
                if b == 0:
                    split_q(0, 0)
            split_q(0, 1)
            nc.vector.tensor_copy(ones_a[:], c("ones_a"))
            nc.vector.tensor_copy(ones_b[:], c("ones_b"))
            nc.vector.memset(tri16[:, 1, :], 1.0)
            nc.vector.tensor_copy(tri16[:, 0, :], c("tri"))
            dve.wait_ge(s_sel, 16)
            nc.vector.tensor_copy(sel[:].rearrange("p a n -> p (a n)"), sel_f).then_inc(cst_ready, 1)
            for h in range(2):
                for i in range(BLK):
                    reduce_max(0, h, i)
            mask_v = c("mask_v").rearrange("p (k h) -> p k h", h=HH)
            vb5 = vb[:].rearrange("p b a k (h w) -> p b a k h w", w=VW)
            for n in range(BATCH * CH):
                b, k = n // CH, n % CH
                dve.wait_ge(v_ps, n + 1)
                for h in range(2):
                    last = nc.vector.tensor_tensor(
                        vb5[0:CLEN[k], b, h, k, :, 0:DH],
                        pV[0:CLEN[k], n % 2, h * P:(h + 1) * P].rearrange("p (h w) -> p h w", w=DH),
                        mask_v[0:CLEN[k], k, :].unsqueeze(2).broadcast_to([CLEN[k], HH, DH]), ALU.mult)
                last.then_inc(v_ready, 1)
            for b in range(BATCH):
                for h in range(2):
                    last = nc.vector.tensor_copy(vb5[:, b, h, :, :, DH], mask_v)
            last.then_inc(v_ready, 1)
            dve.wait_ge(wo_h, 1)
            nc.vector.tensor_tensor(wo_lo[:].rearrange("p k n -> p (k n)"), stage[:, 1, :],
                                    wo_hi[:].rearrange("p k n -> p (k n)").bitcast(F32),
                                    ALU.subtract).then_inc(wo_ready, 1)
            dve.wait_ge(bo_ps, 1)
            dve.wait_ge(s_brow, 32)
            link(nc.vector.tensor_tensor(brow[0:1, 1, :], pV[0:1, 0, 0:D], brow[0:1, 0, :], ALU.add))
            dve.wait_ge(m_zero, 1)
            link(nc.vector.tensor_copy(obias[0:1, :], brow[0:1, 1, :]))
            nc.vector.tensor_tensor(obias[32:33, :], brow[0:1, 1, :], obias[0:1, :].bitcast(F32),
                                    ALU.subtract).then_inc(ob_ready, 1)
            dve.wait_ge(s_x[1], 16)
            stats(0, xs(1), var1)
            norm1(1)

            for b in range(BLOCKS + 2):
                nxt, prev = b + 1 < BLOCKS, 1 <= b <= BLOCKS
                if prev:
                    normalise_attention(b - 1, 1)
                if nxt:
                    split_z(b + 1)
                if b >= 2:
                    take_logits(b - 2)
                if nxt:
                    split_q(b + 1, 0)
                    for i in range(3):
                        reduce_max(b + 1, 0, i)
                    split_q(b + 1, 1)
                    reduce_max(b + 1, 0, 3)
                if prev:
                    split_c(b - 1)
                if nxt:
                    reduce_max(b + 1, 1, 0)
                    reduce_max(b + 1, 1, 1)
                if prev:
                    residual(b - 1)
                if nxt:
                    reduce_max(b + 1, 1, 2)
                    reduce_max(b + 1, 1, 3)
                if b < BLOCKS:
                    normalise_attention(b, 0)
                if prev:
                    norm2(b - 1)
                if b + 2 < BLOCKS:
                    dve.wait_ge(s_x[b + 2], 16)
                    stats(0, xs(b + 2), var1)
                    norm1(b + 2)

            def over_e(t):
                return t.unsqueeze(2).broadcast_to([P, TILES, E])

            dve.wait_ge(lg_ready, BLOCKS)
            link(nc.vector.tensor_reduce(red1[:], lg[:], AX_X, ALU.max))
            nc.vector.tensor_tensor(pr[:], lg[:], over_e(red1[:]), ALU.subtract).then_inc(dif_ready, 1)
            dve.wait_ge(e_ready, 1)
            link(nc.vector.tensor_reduce(red1[:], tmp[:], AX_X, ALU.add))
            link(nc.vector.reciprocal(red2[:], red1[:]))
            link(nc.vector.tensor_tensor(pr[:], tmp[:], over_e(red2[:]), ALU.mult))
            e8 = c("iota_e8").unsqueeze(1).broadcast_to([P, TILES, E])
            for k, hot in enumerate((m1, m2)):
                link(nc.vector.tensor_reduce(ptop[:, k, :], pr[:], AX_X, ALU.max))
                link(nc.vector.tensor_tensor(tmp[:], pr[:], over_e(ptop[:, k, :]), ALU.is_equal))
                link(nc.vector.tensor_tensor(tmp[:], tmp[:], e8, ALU.mult))
                link(nc.vector.tensor_reduce(red1[:], tmp[:], AX_X, ALU.min))
                link(nc.vector.tensor_tensor(hot[:], e8, over_e(red1[:]), ALU.is_equal))
                if k == 0:
                    link(nc.vector.scalar_tensor_tensor(out=pr[:], in0=hot[:], scalar=-2.0, in1=pr[:],
                                                        op0=ALU.mult, op1=ALU.add))
            nc.vector.tensor_tensor(m16[:], m1[:], m2[:], ALU.add).then_inc(m_done, 1)
            dve.wait_ge(rank_ps, 1)
            link(nc.vector.tensor_copy(cnt[:], pM[:, 1, 0:P].rearrange("p (t e) -> p e t", e=E)))
            link(nc.vector.tensor_tensor_scan(inc[:].rearrange("p e t -> p (e t)"), c("not_first"),
                                              cnt[:].rearrange("p e t -> p (e t)"), 0.0, ALU.mult, ALU.add))
            link(nc.vector.tensor_scalar(nt_i[:], inc[:, :, TILES - 1], float(P - 1), None, ALU.add))
            link(nc.vector.tensor_scalar(nt_s[:], nt_i[:], 7, None, ALU.logical_shift_right))
            link(nc.vector.tensor_copy(nt[:], nt_s[:]))
            link(nc.vector.tensor_tensor_scan(ends[:], c("ones_e"), nt[:], 0.0, ALU.mult, ALU.add))
            link(nc.vector.tensor_tensor(starts[:], ends[:], nt[:], ALU.subtract))
            link(nc.vector.tensor_tensor(base[:], inc[:], cnt[:], ALU.subtract))
            link(nc.vector.scalar_tensor_tensor(out=base[:], in0=starts[:].unsqueeze(2).broadcast_to([P, E, TILES]),
                                                scalar=float(P), in1=base[:], op0=ALU.mult, op1=ALU.add))
            link(nc.vector.tensor_tensor(pos3[:], pM[:, 0, 0:P].rearrange("p (t e) -> p t e", e=E),
                                         base[:].rearrange("p e t -> p t e"), ALU.add))
            for k, hot in enumerate((m1, m2)):
                last = nc.vector.tensor_tensor(seli[:, k, :, :], pos3[:], hot[:], ALU.mult)
            link(last)
            link(nc.vector.tensor_reduce(pos[:], seli[:].rearrange("p k t e -> p (k t) e"), AX_X, ALU.add))
            link(nc.vector.tensor_copy(pos_i[:], pos[:]))
            nc.vector.tensor_scalar(pa_i[:], pos_i[:], 7, None, ALU.logical_shift_right)
            link(nc.vector.tensor_scalar(pb_i[:], pos_i[:], P - 1, None, ALU.bitwise_and))
            nc.vector.tensor_copy(pa[:], pa_i[:])
            link(nc.vector.tensor_copy(pb[:], pb_i[:]))
            q = TOPK * TILES
            link(nc.vector.tensor_tensor(hot_a[:], c("iota_t").unsqueeze(1).broadcast_to([P, q, NT]),
                                         pa[:].unsqueeze(2).broadcast_to([P, q, NT]), ALU.is_equal))
            for k in range(TOPK):
                sl = slice(k * TILES, (k + 1) * TILES)
                nc.vector.tensor_tensor(val_a[:, sl, :], hot_a[:, sl, :],
                                        c("tok1").unsqueeze(2).broadcast_to([P, TILES, NT]), ALU.mult)
            for g in range(4):
                sl = slice(g * q // 4, (g + 1) * q // 4)
                nc.vector.tensor_tensor(hot_b[:, sl, :], c("iota_p").unsqueeze(1).broadcast_to([P, q // 4, P]),
                                        pb[:, sl].unsqueeze(2).broadcast_to([P, q // 4, P]),
                                        ALU.is_equal).then_inc(hot_ready, 1)
            link(nc.vector.tensor_tensor(le[:], c("iota_t")[0:1, :].unsqueeze(2).broadcast_to([1, NT, E]),
                                         ends[0:1, :].unsqueeze(1).broadcast_to([1, NT, E]), ALU.is_ge))
            link(nc.vector.tensor_reduce(ex_f[:], le[:], AX_X, ALU.add))
            nc.vector.tensor_scalar(ex_i[:], ex_f[:], float(E - 1), None, ALU.min).then_inc(ex_ready, 1)
            dve.wait_ge(tab_ps, 1)
            link(nc.vector.tensor_copy(tab[:, 0:2, :].rearrange("p a n -> p (a n)"), pG[:, 0, 0:2 * NT]))
            nc.vector.tensor_scalar(tab[:, 3, :], tab[:, 1, :], 0.0, float(TOK), ALU.is_gt, ALU.mult)
            link(nc.vector.tensor_tensor(tab[:, 2, :], tab[:, 0, :], tab[:, 1, :], ALU.add))
            nc.vector.tensor_scalar(src_i[:], tab[:, 2, :], -1.0, 0.0, ALU.add, ALU.max)
            link(nc.vector.scalar_tensor_tensor(out=tab[:, 4, :], in0=tab[:, 2, :], scalar=0.0, in1=c("idle"),
                                                op0=ALU.is_equal, op1=ALU.mult))
            link(nc.vector.tensor_tensor(tab[:, 3, :], tab[:, 3, :], tab[:, 4, :], ALU.add))
            nc.vector.scalar_tensor_tensor(out=dst_i[:], in0=tab[:, 2, :], scalar=-1.0, in1=tab[:, 3, :],
                                           op0=ALU.add, op1=ALU.add).then_inc(idx_ready, 1)

            def x_low(j):
                dve.wait_ge(x_hi, j + 1)
                nc.vector.tensor_tensor(xT_lo[:, j % 2, :], pG[:, j % 2, 0:D], xT_hi[:, j % 2, :].bitcast(F32),
                                        ALU.subtract).then_inc(x_lo, 1)

            def h_low(j):
                dve.wait_ge(h_hi, j + 1)
                nc.vector.tensor_tensor(hT_lo[:, j % 2, :], pS[:, j % 2, 0:D], hT_hi[:, j % 2, :].bitcast(F32),
                                        ALU.subtract).then_inc(h_lo, 1)

            def take_y(j):
                dve.wait_ge(y_ps, j + 1)
                if j >= RING:
                    dve.wait_ge(s_ys[j % RING], 16 * (j // RING))
                nc.vector.tensor_copy(y_sb[:, j % RING, :], pV[:, j % 2, 0:D]).then_inc(y_ready, 1)

            x_low(0)
            for j in range(NT + 1):
                if j >= 1:
                    h_low(j - 1)
                if j + 1 < NT:
                    x_low(j + 1)
                if j >= 1:
                    take_y(j - 1)

            link(nc.vector.tensor_scalar(ptop[:], ptop[:], tg[:, 1:2], None, ALU.mult))
            for b in range(BLOCKS):
                dve.wait_ge(s_yc[b], 16 * TOPK)
                for k in range(TOPK):
                    for i in range(BLK):
                        t = b * BLK + i
                        last = nc.vector.scalar_tensor_tensor(
                            out=x_sb[:, t, :], in0=yc[k][:, t, :], scalar=ptop[:, k, t:t + 1],
                            in1=x_sb[:, t, :], op0=ALU.mult, op1=ALU.add)
                    if k == 0:
                        link(last)
                last.then_inc(out_ready, 1)

        @block.tensor
        def _(pe):
            def product(out, pairs, extra=None):
                for n, (l, r) in enumerate(pairs):
                    last = nc.tensor.matmul(out, l, r, start=(n == 0), stop=(n == len(pairs) - 1))
                return last

            pe.wait_ge(s_ctx, 16)
            pe.wait_ge(s_wkv, 16)
            pe.wait_ge(s_wkv, 32)
            for h in range(2):
                product(pS[:, h, 0:2 * KV], [(wk_sb[:, k, h * P:(h + 1) * P], ctxT[:, k, :])
                                             for k in range(2)]).then_inc(k_ps, 1)

            def transpose_z(b):
                pe.wait_ge(z_ready, b + 1)
                if b == 0:
                    pe.wait_ge(s_cst, 16)
                if b >= 3:
                    pe.wait_ge(z2T_ready, b - 2)
                elif b == 2:
                    pe.wait_ge(q_lo, 4)
                elif b == 1:
                    pe.wait_ge(q_lo, 2)
                for k in range(2):
                    for i in range(BLK):
                        last = nc.tensor.transpose(pG[:, k, i * P:(i + 1) * P],
                                                   z_sb[:, i, k * P:(k + 1) * P], ident)
                last.then_inc(zT_ps, 1)

            def make_q(b, h):
                pe.wait_ge(z_lo, b + 1)
                if b == 0:
                    pe.wait_ge(wq_ready, 1)
                cols = slice(h * P, (h + 1) * P)
                product(pG[:, h, :], [(w[:, k, cols], z[:, k, :]) for k in range(2) for w, z in
                                      ((wq_hi, zq_hi), (wq_hi, zq_lo), (wq_lo, zq_hi))]).then_inc(q_ps, 1)

            def head_scores(b, h, i):
                n = 8 * b + 4 * h + i
                if i == 0:
                    pe.wait_ge(q_hi, 2 * b + h + 1)
                    pe.wait_ge(kb_ready, 8 if b >= 2 else 4)
                if n >= 1:
                    pe.wait_ge(sm_red, n)
                if b >= 1 and h == 0 and i == 0:
                    pe.wait_ge(m_ready, b)
                if b >= 3 and h == 0 and i == 0:
                    pe.wait_ge(lg_ready, b - 2)
                for g in range(2):
                    last = nc.tensor.matmul(pM[:, g, 0:4 * KV], qT_hi[:, unit(b, h), i * P:(i + 1) * P],
                                            kb_hi[:, b // 2, h, g * 4 * KV:(g + 1) * 4 * KV],
                                            start=True, stop=True)
                last.then_inc(sm_ps, 1)

            def transpose_max(b):
                pe.wait_ge(sm_red, 8 * (b + 1))
                for i in range(BLK):
                    last = nc.tensor.transpose(pM[0:NH, 0, i * P:(i + 1) * P], mx[:, i, :], ident)
                last.then_inc(mT_ps, 1)

            def scores(b, s):
                h, k = s // CH, s % CH
                n = 2 * CH * b + s
                if k == 0:
                    pe.wait_ge(q_lo, 2 * b + h + 1)
                if s == 0:
                    pe.wait_ge(m_ready, b + 1)
                if n == 0:
                    pe.wait_ge(cst_ready, 1)
                if n >= 2:
                    pe.wait_ge(exp_done, n - 1)
                rows = slice(k * CS, k * CS + CLEN[k])
                u, kb = unit(b, h), b // 2
                product(pS[0:CLEN[k], n % 2, :],
                        [(kb_hi[:, kb, h, rows], qT_hi[:, u, :]), (kb_hi[:, kb, h, rows], qT_lo[:, u, :]),
                         (kb_lo[:, kb, h, rows], qT_hi[:, u, :]),
                         (sel[:, h, rows], m_sb[:, b % 2, :])]).then_inc(s_ps, 1)

            def weigh(b, h, i):
                n = 2 * b + h
                if i == 0:
                    pe.wait_ge(exp_done, 2 * CH * b + CH * (h + 1))
                    if n == 0:
                        pe.wait_ge(v_ready, BATCH * CH + 1)
                        pe.wait_ge(ob_ready, 1)
                    else:
                        pe.wait_ge(normed, n)
                off = (i % 2) * 256
                product(pV[:, i // 2, off:off + HH * VW],
                        [(prob[0:CLEN[k], (h * CH + k) * BN + i * P:(h * CH + k) * BN + (i + 1) * P],
                          vb[0:CLEN[k], b // 2, h, k, :]) for k in range(CH)]).then_inc(pv_ps, 1)

            def transpose_c(b):
                pe.wait_ge(normed, 2 * (b + 1))
                pe.wait_ge(q_lo, min(2 * (b + 3), 2 * BLOCKS))
                for k in range(2):
                    for i in range(BLK):
                        last = nc.tensor.transpose(pG[:, k, i * P:(i + 1) * P],
                                                   c_sb[:, i, k * P:(k + 1) * P], ident)
                last.then_inc(cT_ps, 1)

            def project(b):
                pe.wait_ge(c_lo, b + 1)
                if b == 0:
                    pe.wait_ge(ob_ready, 1)
                for i in range(BLK):
                    t = slice(i * P, (i + 1) * P)
                    last = product(pG[:, i // 2, (i % 2) * D:(i % 2 + 1) * D],
                                   [(z[:, k, t], w[:, k, :]) for k in range(2) for z, w in
                                    ((zq_hi, wo_hi), (zq_hi, wo_lo), (zq_lo, wo_hi))]
                                   + [(ones_a[:], obias[:])])
                last.then_inc(o_ps, 1)

            def transpose_z2(b):
                pe.wait_ge(z2_ready, b + 1)
                for k in range(2):
                    for i in range(BLK):
                        last = nc.tensor.transpose(pG[:, k, i * P:(i + 1) * P],
                                                   z2_sb[:, i, k * P:(k + 1) * P], ident)
                last.then_inc(z2T_ps, 1)

            def logits(b):
                pe.wait_ge(z2T_ready, b + 1)
                pe.wait_ge(m_ready, min(b + 3, BLOCKS))
                if b == 0:
                    pe.wait_ge(s_rw, 16)
                for i in range(BLK):
                    last = product(pM[:, 0, i * E:(i + 1) * E],
                                   [(z2T[:, k, i * P:(i + 1) * P], rw[:, k, :]) for k in range(2)])
                last.then_inc(lg_ps, 1)

            zq_hi, zq_lo = zT_hi, zT_lo
            transpose_z(0)
            make_q(0, 0)
            make_q(0, 1)
            pe.wait_ge(rep_ready, 1)
            for h in range(2):
                for i in range(BLK):
                    head_scores(0, h, i)
            for n in range(BATCH * CH):
                b, k = n // CH, n % CH
                if n >= 2:
                    pe.wait_ge(v_ready, n - 1)
                product(pV[0:CLEN[k], n % 2, 0:D],
                        [(ctx_rep[:, kk, b, k * CS:k * CS + CLEN[k]], wv_sb[:, kk, :])
                         for kk in range(2)]).then_inc(v_ps, 1)
            pe.wait_ge(v_ready, BATCH * CH)
            pe.wait_ge(s_wo, 16)
            pe.wait_ge(s_bias, 16)
            product(pV[0:1, 0, 0:D], [(bcol[:, 4 + k:5 + k], stage[:, 1, k * D:(k + 1) * D])
                                      for k in range(2)]).then_inc(bo_ps, 1)
            transpose_max(0)
            for b in range(BLOCKS + 2):
                main, nxt, prev = b < BLOCKS, b + 1 < BLOCKS, 1 <= b <= BLOCKS
                for s in range(2 * CH):
                    if main:
                        scores(b, s)
                    if prev and s in (0, 1):
                        weigh(b - 1, 1, 2 * s)
                        weigh(b - 1, 1, 2 * s + 1)
                    if b >= 2 and s == 0:
                        transpose_z2(b - 2)
                    if nxt and s == 1:
                        transpose_z(b + 1)
                    if b >= 2 and s == 1:
                        logits(b - 2)
                    if nxt and s == 2:
                        make_q(b + 1, 0)
                    if nxt and s >= 3:
                        head_scores(b + 1, (s - 3) // 4, (s - 3) % 4)
                    if nxt and s == 5:
                        make_q(b + 1, 1)
                    if prev and s == 6:
                        transpose_c(b - 1)
                    if prev and s == 8:
                        project(b - 1)
                    if main and s >= 6:
                        weigh(b, 0, s - 6)
                if nxt:
                    head_scores(b + 1, 1, 3)
                    transpose_max(b + 1)

            pe.wait_ge(m_done, 1)
            m = m16[:].rearrange("p t e -> p (t e)")
            nc.tensor.matmul(pM[:, 0, 0:P], tri16[:, 0, :], m, start=True, stop=True)
            nc.tensor.matmul(pM[:, 1, 0:P], tri16[:, 1, :], m, start=True, stop=True).then_inc(rank_ps, 1)
            q = TOPK * TILES
            pe.wait_ge(lg_ready, BLOCKS)
            for n in range(q):
                if n % (q // 4) == 0:
                    pe.wait_ge(hot_ready, n // (q // 4) + 1)
                k = n // TILES
                last = nc.tensor.matmul(pG[:, 0, k * NT:(k + 1) * NT], hot_b[:, n, :], val_a[:, n, :],
                                        start=(n % TILES == 0), stop=(n % TILES == TILES - 1))
            last.then_inc(tab_ps, 1)

            def transpose_x(j):
                pe.wait_ge(s_xg[j % RING], 16 * (j // RING + 1))
                if j >= 2:
                    pe.wait_ge(x_lo, j - 1)
                if j == 0:
                    pe.wait_ge(idx_ready, 1)
                for k in range(2):
                    last = nc.tensor.transpose(pG[:, j % 2, k * P:(k + 1) * P],
                                               xg[:, j % RING, k * P:(k + 1) * P], ident)
                last.then_inc(xT_ps, 1)

            def layer(out, hi, lo, w, e, ones):
                pairs = [(ones[:], btab[:, bass.ds(e * D, D)])]
                for k in range(2):
                    w_h = w_hi[w][:, bass.ds(e * 2 * D + k * D, D)]
                    w_l = w_lo[w][:, bass.ds(e * 2 * D + k * D, D)]
                    cols = slice(k * P, (k + 1) * P)
                    pairs += [(hi[:, cols], w_h), (lo[:, cols], w_h), (hi[:, cols], w_l)]
                return product(out, pairs)

            def first(j, e):
                pe.wait_ge(x_lo, j + 1)
                if j >= 2:
                    pe.wait_ge(h_ready, j - 1)
                layer(pM[:, j % 2, 0:D], xT_hi[:, j % 2, :], xT_lo[:, j % 2, :], 0, e,
                      ones_a).then_inc(h_ps, 1)

            def transpose_h(j):
                pe.wait_ge(h_ready, j + 1)
                if j >= 2:
                    pe.wait_ge(h_lo, j - 1)
                for k in range(2):
                    last = nc.tensor.transpose(pS[:, j % 2, k * P:(k + 1) * P],
                                               h_sb[:, j % 2, k * P:(k + 1) * P], ident)
                last.then_inc(hT_ps, 1)

            def second(j, e):
                pe.wait_ge(h_lo, j + 1)
                if j >= 2:
                    pe.wait_ge(y_ready, j - 1)
                layer(pV[:, j % 2, 0:D], hT_hi[:, j % 2, :], hT_lo[:, j % 2, :], 1, e,
                      ones_b).then_inc(y_ps, 1)

            pe.wait_ge(ex_ready, 1)
            pe.wait_ge(stage_used, 2 * E)
            pe.wait_ge(bst_used, 2)
            expert = {}
            transpose_x(0)
            for j in range(NT + 1):
                if j < NT:
                    expert[j] = nc.tensor.value_load(ex_i[0:1, j:j + 1], min_val=0, max_val=E - 1)
                if j >= 1:
                    transpose_h(j - 1)
                if j + 1 < NT:
                    transpose_x(j + 1)
                if j < NT:
                    first(j, expert[j])
                if j >= 1:
                    second(j - 1, expert[j - 1])


def kernel(**inputs):
    import concourse.bacc as _bacc
    from concourse.bass_utils import run_bass_kernel_spmd as _run

    def rows(name, *shape):
        return np.ascontiguousarray(np.asarray(inputs[name]).reshape(shape))

    def turned(name):
        return np.ascontiguousarray(np.asarray(inputs[name]).T)

    const, place = constants()
    g = [np.asarray(inputs[n]).reshape(1, 1) for n in ("g_xattn", "g_ffn")]
    arrays = {
        "x": rows("x", TOK, D),
        "ctx_t": np.ascontiguousarray(np.asarray(inputs["ctx_1024"]).reshape(BATCH * KV, D).T),
        "wq_t": turned("L0_xattn_Wq"), "wk_t": turned("L0_xattn_Wk"),
        "wv_t": turned("L0_xattn_Wv"), "wo_t": turned("L0_xattn_Wo"),
        "bcol": np.ascontiguousarray(np.concatenate(
            [np.asarray(inputs[f"L0_xattn_b{n}"]).reshape(2, P) for n in "qkv"]).T),
        "bo": rows("L0_xattn_bo", 1, D),
        "gates": np.ascontiguousarray(np.tile(np.concatenate(g, 1), (P, 1))),
        "router": rows("L0_ffn_router_w", D, E),
        "w_in": rows("L0_ffn_w_in", E, D, D), "w_out": rows("L0_ffn_w_out", E, D, D),
        "b_in": rows("L0_ffn_b_in", 1, E * D), "b_out": rows("L0_ffn_b_out", 1, E * D),
        "const": const,
    }
    nc = _bacc.Bacc("TRN2", target_bir_lowering=False, num_devices=1)
    aps = {n: nc.dram_tensor(f"in_{n}", v.shape, mybir.dt.from_np(v.dtype), kind="ExternalInput").ap()
           for n, v in arrays.items()}
    aps["out"] = nc.dram_tensor("out_0", (TOK, D), F32, kind="ExternalOutput").ap()
    build(nc, aps, place)
    r = _run(nc, [{f"in_{n}": v for n, v in arrays.items()}], core_ids=[0])
    return r.results[0]["out_0"].reshape(BATCH, SEQ, D)
```

```python
from contextlib import ExitStack

import numpy as np

import concourse.bass as bass
from concourse import mybir

F32 = mybir.dt.float32
F32R = mybir.dt.float32r
F16 = mybir.dt.float16
I32 = mybir.dt.int32
U32 = mybir.dt.uint32
ALU = mybir.AluOpType
ACT = mybir.ActivationFunctionType
AX_X = mybir.AxisListType.X

P = 128
BATCH, SEQ, D = 2, 1024, 256
KV, NH, DH = 77, 16, 16
E, TOPK = 8, 2
TOK = BATCH * SEQ
TILES = TOK // P
BLK = 4
BLOCKS = TILES // BLK
BN = BLK * P
HH = NH // 2
HALF = HH * KV
CH = 5
CS = HALF // CH
CLEN = [CS] * (CH - 1) + [HALF - CS * (CH - 1)]
VW = DH + 1
HT = TILES // BATCH
PAIRS = SEQ * TOPK
NT = (PAIRS - E) // P + E
ALL = BATCH * NT
Q = TOPK * HT
XRING = 8
YRING = 4
EPS = 1e-5


def constants():
    p = np.arange(P)
    parts = {
        "ident": np.eye(P),
        "tri": (p[:, None] < p[None, :]),
        "mask_k": (p[:, None] // DH == np.arange(HH)[None, :]),
        "mask_v": np.stack([(CS * k + p)[:, None] // KV == np.arange(HH) for k in range(CH)], 1),
        "iota_p": np.broadcast_to(p, (P, P)),
        "iota_t": np.broadcast_to(np.arange(NT), (P, NT)),
        "iota_e8": np.broadcast_to(np.arange(E) - E, (P, E)),
        "not_first": np.broadcast_to(np.arange(E * HT) % HT != 0, (P, E * HT)),
        "ones_e": np.ones((P, E)),
        "tok1": p[:, None] + P * np.arange(HT)[None, :] + 1,
        "idle": PAIRS + 1 + p[:, None] + P * np.arange(NT)[None, :],
        "ones_a": np.broadcast_to(((p == 0) | (p == 32))[:, None], (P, P)),
        "ones_b": np.broadcast_to(((p == 64) | (p == 96))[:, None], (P, P)),
        "sel": p[:, None] == (HH * np.arange(2)[:, None] + np.arange(HALF) // KV).reshape(1, -1),
    }
    place, cols, at = {}, [], 0
    for name, a in parts.items():
        a = np.asarray(a, np.float32).reshape(P, -1)
        place[name] = (at, at + a.shape[1])
        at += a.shape[1]
        cols.append(a)
    return np.ascontiguousarray(np.concatenate(cols, 1)), place


def build(nc, a, place):
    ctx = ExitStack()
    with ctx:
        early, late = ExitStack(), ExitStack()

        def sb(name, shape, dt, st=ctx):
            return st.enter_context(nc.sbuf_tensor(name, shape, dt))

        def sem(name):
            return ctx.enter_context(nc.semaphore(name))

        n_small = place["sel"][0]
        x_sb = sb("x_sb", [P, TILES, D], F32)
        cst = sb("cst", [P, n_small], F32)
        gates_in = sb("gates_in", [P, 2], F32)
        tg = sb("tg", [P, 2], F32)
        w_hi = [sb(f"w{n}_hi", [P, E * 2 * D], F32R) for n in ("in", "out")]
        w_lo = [sb(f"w{n}_lo", [P, E * 2 * D], F32R) for n in ("in", "out")]
        btab = sb("btab", [P, E * D], F32R)
        ones_a = sb("ones_a", [P, P], F32R)
        ones_b = sb("ones_b", [P, P], F32R)
        tri16 = sb("tri16", [P, 2, P], F16)
        lg = sb("lg", [P, TILES, E], F32)

        zT_hi = sb("zT_hi", [P, 2, BN], F32R)
        zT_lo = sb("zT_lo", [P, 2, BN], F32R)
        c_sb = sb("c_sb", [P, BLK, D], F32)
        wo_hi = sb("wo_hi", [P, 2, D], F32R)
        wo_lo = sb("wo_lo", [P, 2, D], F32R)
        obias = sb("obias", [P, D], F32R)
        stage = sb("stage", [P, 2, 2 * D], F32)
        bcol = sb("bcol", [P, 6], F32)
        brow = sb("brow", [1, D], F32)
        mx = sb("mx", [P, BLK, NH], F32)
        st6 = sb("st6", [P, 2, BLK, 6], F32)
        mv = sb("mv", [P, 2, BLK, 2], F32)
        rstd = sb("rstd", [P, 2, BLK], F32)
        veps = sb("veps", [P, 2, BLK], F32)
        half = sb("half", [P, BLK], F32)
        rden = sb("rden", [P, BLK, HH], F32)
        z2T = sb("z2T", [P, 2, BN], F32)
        rw = sb("rw", [P, 2, E], F32)
        z2_sb = sb("z2_sb", [P, BLK, D], F32)
        ptop = sb("ptop", [P, TOPK, TILES], F32)
        src_i = sb("src_i", [P, ALL], U32)
        dst_i = sb("dst_i", [P, ALL], U32)
        ex_i = sb("ex_i", [1, ALL], I32)

        wq_hi = sb("wq_hi", [P, 2, D], F32R, early)
        wq_lo = sb("wq_lo", [P, 2, D], F32R, early)
        z_sb = sb("z_sb", [P, BLK, D], F32, early)
        kT = sb("kT", [P, 2, 2 * KV], F32, early)
        kT_hi = sb("kT_hi", [P, 2, 2 * KV], F32, early)
        kT_lo = sb("kT_lo", [P, 2, 2 * KV], F32, early)
        kb_hi = sb("kb_hi", [P, BATCH, 2, HALF], F32R, early)
        kb_lo = sb("kb_lo", [P, BATCH, 2, HALF], F32R, early)
        sel = sb("sel", [P, 2, HALF], F32R, early)
        qT_hi = sb("qT_hi", [P, 3, BN], F32R, early)
        qT_lo = sb("qT_lo", [P, 3, BN], F32R, early)
        m_sb = sb("m_sb", [P, 2, BN], F32R, early)
        vb = sb("vb", [P, BATCH, 2, CH, HH * VW], F32, early)
        prob = sb("prob", [P, 2 * CH * BN], F32, early)
        at = [0]

        def setup_view(n):
            at[0] += n
            return prob[:, at[0] - n:at[0]]

        ctxT = setup_view(2 * 2 * KV).rearrange("p (k n) -> p k n", k=2)
        ctx_rep = setup_view(2 * 2 * HALF).rearrange("p (k b n) -> p k b n", k=2, b=2)
        wk_sb = setup_view(2 * D).rearrange("p (k n) -> p k n", k=2)
        wv_sb = setup_view(2 * D).rearrange("p (k n) -> p k n", k=2)
        sel_f = setup_view(2 * HALF)
        early.close()

        def mo(name, shape, dt):
            return sb(name, shape, dt, late)

        pr = mo("pr", [P, HT, E], F32)
        tmp = mo("tmp", [P, HT, E], F32)
        m1 = mo("m1", [P, HT, E], F32)
        m2 = mo("m2", [P, HT, E], F32)
        m16 = mo("m16", [P, HT, E], F16)
        red1 = mo("red1", [P, HT], F32)
        red2 = mo("red2", [P, HT], F32)
        cnt = mo("cnt", [P, E, HT], F32)
        inc = mo("inc", [P, E, HT], F32)
        base = mo("base", [P, E, HT], F32)
        pos3 = mo("pos3", [P, HT, E], F32)
        seli = mo("seli", [P, TOPK, HT, E], F32)
        pos = mo("pos", [P, Q], F32)
        pos_i = mo("pos_i", [P, Q], I32)
        pa_i = mo("pa_i", [P, Q], I32)
        pb_i = mo("pb_i", [P, Q], I32)
        pa = mo("pa", [P, Q], F32)
        pb = mo("pb", [P, Q], F32)
        nt_i = mo("nt_i", [P, E], I32)
        nt_s = mo("nt_s", [P, E], I32)
        nt = mo("nt", [P, E], F32)
        ends = mo("ends", [P, E], F32)
        starts = mo("starts", [P, E], F32)
        le = mo("le", [1, NT, E], F32)
        ex_f = mo("ex_f", [1, NT], F32)
        hot_b = mo("hot_b", [P, Q, P], F16)
        hot_a = mo("hot_a", [P, Q, NT], F32)
        val_a = mo("val_a", [P, Q, NT], F16)
        tab = mo("tab", [P, 5, NT], F32)
        xg = mo("xg", [P, XRING, D], F32)
        xT_hi = mo("xT_hi", [P, 2, D], F32R)
        xT_lo = mo("xT_lo", [P, 2, D], F32R)
        h_sb = mo("h_sb", [P, 2, D], F32)
        hT_hi = mo("hT_hi", [P, 2, D], F32R)
        hT_lo = mo("hT_lo", [P, 2, D], F32R)
        y_sb = mo("y_sb", [P, YRING, D], F32)
        yc = [mo(f"yc{k}", [P, TILES, D], F32) for k in range(TOPK)]
        late.close()

        def pair(name):
            return ctx.enter_context(nc.psum_tensor(name, [P, 2, 512], F32))

        pG = pair("pG")
        pM = pair("pM")
        pS = pair("pS")
        pV = pair("pV")
        pL = [pM, pM, pG, pG]
        pR = [pM, pG]

        z_dram = [nc.dram_tensor(f"z_dram{n}", [SEQ, D], F32, kind="Internal").ap() for n in range(BATCH)]
        y_dram = [nc.dram_tensor(f"y_dram{n}", [PAIRS + NT * P, D], F32, kind="Internal").ap()
                  for n in range(BATCH)]

        s_x = [sem(f"s_x{b}") for b in range(BLOCKS)]
        s_ctx, s_wk, s_wv, s_cst, s_sel = sem("s_ctx"), sem("s_wk"), sem("s_wv"), sem("s_cst"), sem("s_sel")
        s_wq, s_wo, s_bias, s_brow, s_rw = sem("s_wq"), sem("s_wo"), sem("s_bias"), sem("s_brow"), sem("s_rw")
        s_stage = [sem("s_stage0"), sem("s_stage1")]
        s_bst = [sem("s_bst0"), sem("s_bst1")]
        s_zd = [sem(f"s_zd{b}") for b in range(BLOCKS)]
        s_xg = [sem(f"s_xg{r}") for r in range(XRING)]
        s_ys = [sem(f"s_ys{r}") for r in range(YRING)]
        s_yc = [sem(f"s_yc{b}") for b in range(BLOCKS)]
        s_out = sem("s_out")
        dve_step, pool_step, act_step = sem("dve_step"), sem("pool_step"), sem("act_step")
        rep_ready, wq_h, wo_h, tg_ready = sem("rep_ready"), sem("wq_h"), sem("wo_h"), sem("tg_ready")
        wq_ready, wo_ready = sem("wq_ready"), sem("wo_ready")
        k_ps, kt_ready, v_ps, v_ready = sem("k_ps"), sem("kt_ready"), sem("v_ps"), sem("v_ready")
        kh_ready, kl_ready, k1_ready = sem("kh_ready"), sem("kl_ready"), sem("k1_ready")
        bo_ps, ob_ready, cst_ready, m_zero = sem("bo_ps"), sem("ob_ready"), sem("cst_ready"), sem("m_zero")
        bst_zero, bst_used, btab_ready, stage_used = sem("bst_zero"), sem("bst_used"), sem("btab_ready"), sem("stage_used")
        var1, var2, rstd1, rstd2 = sem("var1"), sem("var2"), sem("rstd1"), sem("rstd2")
        z_ready, zT_ps, z_hi, z_lo = sem("z_ready"), sem("zT_ps"), sem("z_hi"), sem("z_lo")
        q_ps, q_hi, q_lo = sem("q_ps"), sem("q_hi"), sem("q_lo")
        sm_ps, sm_red, mT_ps, m_ready = sem("sm_ps"), sem("sm_red"), sem("mT_ps"), sem("m_ready")
        s_ps, exp_done, pv_ps, normed = sem("s_ps"), sem("exp_done"), sem("pv_ps"), sem("normed")
        cT_ps, c_hi, c_lo, o_ps = sem("cT_ps"), sem("c_hi"), sem("c_lo"), sem("o_ps")
        x1_ready, z2_ready, z2T_ps, z2T_ready = sem("x1_ready"), sem("z2_ready"), sem("z2T_ps"), sem("z2T_ready")
        lg_ps, lg_ready = sem("lg_ps"), sem("lg_ready")
        dif_ready, e_ready, m_done, rank_ps = sem("dif_ready"), sem("e_ready"), sem("m_done"), sem("rank_ps")
        hot_ready, tab_ps, ex_ready, idx_ready = sem("hot_ready"), sem("tab_ps"), sem("ex_ready"), sem("idx_ready")
        xT_ps, x_hi, x_lo = sem("xT_ps"), sem("x_hi"), sem("x_lo")
        h_ps, h_ready, hT_ps, h_hi, h_lo = sem("h_ps"), sem("h_ready"), sem("hT_ps"), sem("h_hi"), sem("h_lo")
        y_ps, y_ready, out_ready = sem("y_ps"), sem("y_ready"), sem("out_ready")

        def c(name):
            lo, hi = place[name]
            return cst[:, lo:hi]

        ident = c("ident")
        x_t = a["x"].rearrange("(b t p) d -> b p t d", p=P, t=BLK)
        out_t = a["out"].rearrange("(b t p) d -> b p t d", p=P, t=BLK)
        z_t = [z.rearrange("(b t p) d -> b p t d", p=P, t=BLK) for z in z_dram]
        y_t = [y[0:PAIRS, :].rearrange("(k b t p) d -> k b p t d", p=P, t=BLK, k=TOPK) for y in y_dram]

        def unit(blk, half):
            return (2 * blk + half) % 3

        block = ctx.enter_context(nc.Block())

        @block.sync
        def _(sp):
            def two(w):
                return w.rearrange("(k p) n -> p k n", p=P)

            sp.dma_start(x_sb[:, 0:BLK, :], x_t[0]).then_inc(s_x[0], 16)
            sp.dma_start(ctxT, two(a["ctx_t"])).then_inc(s_ctx, 16)
            sp.dma_start(wk_sb, two(a["wk_t"])).then_inc(s_wk, 16)
            sp.dma_start(cst[:], a["const"][:, 0:n_small]).then_inc(s_cst, 16)
            sp.dma_start(bcol[:], a["bcol"]).then_inc(s_bias, 16)
            sp.dma_start(stage[:, 0, :].rearrange("p (k n) -> p k n", k=2), two(a["wq_t"])).then_inc(s_wq, 16)
            sp.dma_start(wv_sb, two(a["wv_t"])).then_inc(s_wv, 16)
            sp.dma_start(sel_f, a["const"][:, n_small:]).then_inc(s_sel, 16)
            sp.dma_start(x_sb[:, BLK:2 * BLK, :], x_t[1]).then_inc(s_x[1], 16)
            sp.dma_start(stage[:, 1, :].rearrange("p (k n) -> p k n", k=2), two(a["wo_t"])).then_inc(s_wo, 16)
            sp.dma_start(brow[0:1, :], a["bo"]).then_inc(s_brow, 16)
            sp.dma_start(gates_in[:], a["gates"]).then_inc(s_brow, 16)
            sp.dma_start(rw[:], a["router"].rearrange("(k p) e -> p k e", p=P)).then_inc(s_rw, 16)
            for b in range(2, BLOCKS):
                sp.dma_start(x_sb[:, b * BLK:(b + 1) * BLK, :], x_t[b]).then_inc(s_x[b], 16)
            for g in range(2):
                sp.wait_ge(bst_zero, 1)
                if g:
                    sp.wait_ge(bst_used, 1)
                for row, name in ((0, "b_in"), (32, "b_in"), (64, "b_out"), (96, "b_out")):
                    sp.dma_start(z2_sb[row:row + 1, :, :].rearrange("p e d -> p (e d)"),
                                 a[name][:, g * BLK * D:(g + 1) * BLK * D]).then_inc(s_bst[g], 16)
            sp.wait_ge(wq_ready, 1)
            for u in range(2 * E):
                e, which = u // 2, u % 2
                if u == 1:
                    sp.wait_ge(wo_ready, 1)
                    sp.wait_ge(bo_ps, 1)
                if u >= 2:
                    sp.wait_ge(stage_used, u - 1)
                w = a["w_out" if which else "w_in"]
                sp.dma_start(stage[:, u % 2, :].rearrange("p (k n) -> p k n", k=2),
                             w[e].rearrange("(k p) n -> p k n", p=P)).then_inc(s_stage[u % 2], 16)
            for n in range(BATCH):
                for r in range(YRING):
                    sp.wait_ge(s_ys[r], 16 * len(range(r, (n + 1) * NT, YRING)))
                for b in range(n * 2, n * 2 + 2):
                    for k in range(TOPK):
                        sp.dma_start(yc[k][:, b * BLK:(b + 1) * BLK, :], y_t[n][k, b % 2]).then_inc(s_yc[b], 16)
                for b in range(n * 2, n * 2 + 2):
                    sp.wait_ge(out_ready, b + 1)
                    sp.dma_start(out_t[b], x_sb[:, b * BLK:(b + 1) * BLK, :]).then_inc(s_out, 16)
            sp.wait_ge(s_out, 16 * BLOCKS)

        @block.gpsimd
        def _(pool):
            step = [0]

            def link(ins):
                step[0] += 1
                ins.then_inc(pool_step, 1)
                pool.wait_ge(pool_step, step[0])

            def inv_std(which, n, src, done):
                pool.wait_ge(src, n + 1)
                link(nc.gpsimd.tensor_scalar(veps[:, which, :], mv[:, which, :, 1], EPS, None, ALU.add))
                nc.gpsimd.tensor_tensor(rstd[:, which, :], veps[:, which, :], half[:],
                                        ALU.pow).then_inc(done, 1)

            def split_weights(u0, u1):
                for u in range(u0, u1):
                    e, which = u // 2, u % 2
                    sl = slice(e * 2 * D, (e + 1) * 2 * D)
                    pool.wait_ge(s_stage[u % 2], 16 * (u // 2 + 1))
                    link(nc.gpsimd.tensor_copy(w_hi[which][:, sl], stage[:, u % 2, :]))
                    nc.gpsimd.tensor_tensor(w_lo[which][:, sl], stage[:, u % 2, :],
                                            w_hi[which][:, sl].bitcast(F32),
                                            ALU.subtract).then_inc(stage_used, 1)

            nc.gpsimd.memset(z2_sb[:], 0.0).then_inc(bst_zero, 1)
            link(nc.gpsimd.memset(half[:], -0.5))
            nc.gpsimd.memset(obias[:].bitcast(F32), 0.0).then_inc(m_zero, 1)
            nc.gpsimd.memset(m_sb[:].bitcast(F32), 0.0).then_inc(m_zero, 1)
            def key_blocks(b, part, dst, done):
                for h in range(2):
                    nc.gpsimd.tensor_tensor(
                        dst[:, b, h, :].rearrange("p (h n) -> p h n", n=KV),
                        part[:, h, b * KV:(b + 1) * KV].unsqueeze(1).broadcast_to([P, HH, KV]),
                        c("mask_k").unsqueeze(2).broadcast_to([P, HH, KV]), ALU.mult).then_inc(done, 1)

            inv_std(0, 0, var1, rstd1)
            pool.wait_ge(wq_h, 1)
            nc.gpsimd.tensor_tensor(wq_lo[:].rearrange("p k n -> p (k n)"), stage[:, 0, :],
                                    wq_hi[:].rearrange("p k n -> p (k n)").bitcast(F32),
                                    ALU.subtract).then_inc(wq_ready, 1)
            pool.wait_ge(s_cst, 16)
            pool.wait_ge(kt_ready, 1)
            key_blocks(0, kT_lo, kb_lo, kl_ready)
            inv_std(0, 1, var1, rstd1)
            key_blocks(1, kT_hi, kb_hi, k1_ready)
            key_blocks(1, kT_lo, kb_lo, k1_ready)
            for g in range(2):
                pool.wait_ge(s_bst[g], 64)
                sl = slice(g * BLK * D, (g + 1) * BLK * D)
                src = z2_sb[:].rearrange("p e d -> p (e d)")
                link(nc.gpsimd.tensor_copy(btab[:, sl], src))
                for row in (32, 96):
                    last = nc.gpsimd.tensor_tensor(btab[row:row + 1, sl], src[row:row + 1, :],
                                                   btab[row:row + 1, sl].bitcast(F32), ALU.subtract)
                    if row == 32:
                        link(last)
                last.then_inc(bst_used, 1)
                pool.wait_ge(bst_used, g + 1)
                if g == 0:
                    inv_std(0, 2, var1, rstd1)
            split_weights(0, 4)
            inv_std(0, 3, var1, rstd1)
            split_weights(4, 7)
            inv_std(1, 0, var2, rstd2)
            split_weights(7, 12)
            inv_std(1, 1, var2, rstd2)
            split_weights(12, 2 * E)

            def gather(j):
                r, n = j % XRING, j // NT
                if j % NT == 0:
                    for b in range(2 * n, 2 * n + 2):
                        pool.wait_ge(s_zd[b], 16)
                    pool.wait_ge(idx_ready, n + 1)
                if j >= XRING:
                    pool.wait_ge(xT_ps, j - XRING + 1)
                if j == 0:
                    pool.wait_ge(s_ps, 2 * CH * BLOCKS)
                pool.indirect_dma_start(
                    out=xg[:, r, :], out_offset=None, in_=z_dram[n],
                    in_offset=bass.IndirectOffsetOnAxis(ap=src_i[:, j:j + 1], axis=0),
                ).then_inc(s_xg[r], 16)

            def scatter(j):
                r = j % YRING
                pool.wait_ge(y_ready, j + 1)
                pool.indirect_dma_start(
                    out=y_dram[j // NT], out_offset=bass.IndirectOffsetOnAxis(ap=dst_i[:, j:j + 1], axis=0),
                    in_=y_sb[:, r, :], in_offset=None,
                ).then_inc(s_ys[r], 16)

            for j in range(XRING):
                gather(j)
                if j == 1:
                    inv_std(1, 2, var2, rstd2)
            for j in range(ALL):
                scatter(j)
                if j == 2:
                    inv_std(1, 3, var2, rstd2)
                if j + XRING < ALL:
                    gather(j + XRING)

        @block.scalar
        def _(act):
            act.wait_ge(s_ctx, 16)
            for k in range(2):
                for b in range(BATCH):
                    last = nc.scalar.activation(
                        ctx_rep[:, k, b, :].rearrange("p (h n) -> p h n", h=HH),
                        ctxT[:, k, b * KV:(b + 1) * KV].unsqueeze(1).broadcast_to([P, HH, KV]), ACT.Copy)
            last.then_inc(rep_ready, 1)
            act.wait_ge(s_wq, 16)
            nc.scalar.activation(wq_hi[:].rearrange("p k n -> p (k n)"), stage[:, 0, :], ACT.Copy).then_inc(wq_h, 1)
            def split_z(b):
                act.wait_ge(zT_ps, 2 * b + 2)
                if b >= 3:
                    act.wait_ge(o_ps, b - 2)
                for k in range(2):
                    nc.scalar.activation(zT_hi[:, k, :], pG[:, k, :], ACT.Copy).then_inc(z_hi, 1)

            def split_q(b, h):
                act.wait_ge(q_ps, 2 * b + h + 1)
                if 2 * b + h >= 3:
                    act.wait_ge(s_ps, CH * (2 * b + h - 2))
                nc.scalar.activation(qT_hi[:, unit(b, h), :], pG[:, h, :], ACT.Identity,
                                     bias=bcol[:, h:h + 1]).then_inc(q_hi, 1)

            def negate_max(b):
                act.wait_ge(mT_ps, b + 1)
                if b >= 2:
                    act.wait_ge(s_ps, 2 * CH * (b - 1))
                nc.scalar.activation(m_sb[0:NH, b % 2, :], pM[0:NH, 0, :], ACT.Copy,
                                     scale=-1.0).then_inc(m_ready, 1)

            def exp(b, s):
                h, k = s // CH, s % CH
                n = 2 * CH * b + s
                act.wait_ge(s_ps, n + 1)
                if b >= 1 and k == 0:
                    act.wait_ge(pv_ps, BLK * (2 * (b - 1) + h + 1))
                nc.scalar.activation(prob[0:CLEN[k], s * BN:(s + 1) * BN], pS[0:CLEN[k], n % 2, :],
                                     ACT.Exp).then_inc(exp_done, 1)

            def split_c(b):
                act.wait_ge(cT_ps, b + 1)
                act.wait_ge(q_ps, min(2 * (b + 3), 2 * BLOCKS))
                nc.scalar.activation(zT_hi[:], pG[:], ACT.Copy).then_inc(c_hi, 1)

            def copy_z2(b):
                act.wait_ge(z2T_ps, b + 1)
                if b >= 1:
                    act.wait_ge(lg_ps, b)
                nc.scalar.activation(z2T[:], pL[b][:], ACT.Copy).then_inc(z2T_ready, 1)
                nc.scalar.dma_start(z_t[b // 2][b % 2], z2_sb[:]).then_inc(s_zd[b], 16)

            def router_exp(n):
                act.wait_ge(dif_ready, n + 1)
                nc.scalar.activation(tmp[:], pr[:], ACT.Exp).then_inc(e_ready, 1)

            act.wait_ge(s_bias, 16)
            for b in range(-1, BLOCKS):
                main = b >= 0
                nxt = b + 1 < BLOCKS
                prev = b >= 1
                for s in range(2 * CH):
                    if main:
                        if b == 0 and s == 0:
                            act.wait_ge(v_ps, BATCH * CH)
                            act.wait_ge(cst_ready, 1)
                        exp(b, s)
                    if s == 0 and nxt:
                        split_z(b + 1)
                    if s == 1 and b >= 2:
                        copy_z2(b - 2)
                    if s == 2 and nxt:
                        split_q(b + 1, 0)
                    if s == 5 and nxt:
                        split_q(b + 1, 1)
                    if s == 5 and b == -1:
                        nc.scalar.activation(tri16[:, 0, :], c("tri"), ACT.Copy)
                        nc.scalar.activation(ones_a[:], c("ones_a"), ACT.Copy)
                        nc.scalar.activation(ones_b[:], c("ones_b"), ACT.Copy)
                        act.wait_ge(s_sel, 16)
                        nc.scalar.activation(sel[:].rearrange("p a n -> p (a n)"), sel_f,
                                             ACT.Copy).then_inc(cst_ready, 1)
                        act.wait_ge(s_wo, 16)
                        nc.scalar.activation(wo_hi[:].rearrange("p k n -> p (k n)"), stage[:, 1, :],
                                             ACT.Copy).then_inc(wo_h, 1)
                        act.wait_ge(s_brow, 32)
                        nc.scalar.activation(tg[:], gates_in[:], ACT.Tanh).then_inc(tg_ready, 1)
                    if s == 3 and b == BLOCKS - 1:
                        router_exp(0)
                    if s == 6 and prev:
                        split_c(b - 1)
                if nxt:
                    if b == -1:
                        act.wait_ge(m_zero, 2)
                    negate_max(b + 1)

            def x_high(j):
                act.wait_ge(xT_ps, j + 1)
                if j >= 2:
                    act.wait_ge(h_ps, j - 1)
                nc.scalar.activation(xT_hi[:, j % 2, :], pS[:, 0, 0:D], ACT.Copy).then_inc(x_hi, 1)

            def gelu(j):
                act.wait_ge(h_ps, j + 1)
                if j >= 2:
                    act.wait_ge(hT_ps, j - 1)
                nc.scalar.activation(h_sb[:, j % 2, :], pM[:, j % 2, 0:D],
                                     ACT.Gelu_apprx_tanh).then_inc(h_ready, 1)

            def h_high(j):
                act.wait_ge(hT_ps, j + 1)
                if j >= 2:
                    act.wait_ge(y_ps, j - 1)
                nc.scalar.activation(hT_hi[:, j % 2, :], pS[:, 1, 0:D], ACT.Copy).then_inc(h_hi, 1)

            x_high(0)
            x_high(1)
            for j in range(ALL + 2):
                if j < ALL:
                    gelu(j)
                if 1 <= j <= ALL:
                    h_high(j - 1)
                if j + 2 < ALL:
                    x_high(j + 2)
                if j == 0:
                    copy_z2(2)
                if j == 2:
                    split_c(3)
                if j == 7:
                    copy_z2(3)
                if j == 9:
                    router_exp(1)

        @block.vector
        def _(dve):
            step = [0]

            def link(ins):
                step[0] += 1
                ins.then_inc(dve_step, 1)
                dve.wait_ge(dve_step, step[0])

            def stats(which, src, done):
                for i in range(BLK):
                    last = nc.vector.bn_stats(st6[:, which, i, :], src[:, i, :])
                link(last)
                for i in range(BLK):
                    last = nc.vector.bn_aggr(mv[:, which, i, :], st6[:, which, i, :])
                last.then_inc(done, 1)

            def normalise(which, n, src, dst, inv, done):
                dve.wait_ge(inv, n + 1)
                for i in range(BLK):
                    last = nc.vector.tensor_scalar(dst[:, i, :], src[:, i, :], mv[:, which, i, 0:1],
                                                   rstd[:, which, i:i + 1], ALU.subtract, ALU.mult)
                last.then_inc(done, 1)

            def xs(b):
                return x_sb[:, b * BLK:(b + 1) * BLK, :]

            def norm1(b):
                if b >= 1:
                    dve.wait_ge(zT_ps, 2 * b)
                normalise(0, b, xs(b), z_sb, rstd1, z_ready)

            def split_z(b):
                for k in range(2):
                    dve.wait_ge(z_hi, 2 * b + k + 1)
                    nc.vector.tensor_tensor(zT_lo[:, k, :], pG[:, k, :], zT_hi[:, k, :].bitcast(F32),
                                            ALU.subtract).then_inc(z_lo, 1)

            def split_q(b, h):
                dve.wait_ge(q_hi, 2 * b + h + 1)
                u = unit(b, h)
                nc.vector.scalar_tensor_tensor(out=qT_lo[:, u, :], in0=pG[:, h, :], scalar=bcol[:, h:h + 1],
                                               in1=qT_hi[:, u, :].bitcast(F32), op0=ALU.add,
                                               op1=ALU.subtract).then_inc(q_lo, 1)

            def reduce_max(b, h, i):
                n = 8 * b + 4 * h + i
                if b >= 1 and n % 8 == 0:
                    dve.wait_ge(mT_ps, b)
                for g in range(2):
                    dve.wait_ge(sm_ps, 2 * n + g + 1)
                    nc.vector.tensor_reduce(mx[:, i, h * HH + 4 * g:h * HH + 4 * g + 4],
                                            pM[:, g, 0:4 * KV].rearrange("p (h n) -> p h n", n=KV),
                                            AX_X, ALU.max).then_inc(sm_red, 1)

            def normalise_attention(b, h):
                n = 2 * b + h
                dve.wait_ge(pv_ps, BLK * (n + 1))
                v = pV[:].rearrange("p a (t w) -> p (a t) w", t=2)[:, :, 0:HH * VW].rearrange(
                    "p t (h w) -> p t h w", w=VW)
                link(nc.vector.reciprocal(rden[:], v[:, :, :, DH]))
                if b >= 1 and h == 0:
                    dve.wait_ge(cT_ps, b)
                nc.vector.tensor_tensor(
                    c_sb[:, :, h * P:(h + 1) * P].rearrange("p t (h w) -> p t h w", w=DH),
                    v[:, :, :, 0:DH], rden[:].unsqueeze(3).broadcast_to([P, BLK, HH, DH]),
                    ALU.mult).then_inc(normed, 1)

            def split_c(b):
                dve.wait_ge(c_hi, b + 1)
                nc.vector.tensor_tensor(zT_lo[:], pG[:], zT_hi[:].bitcast(F32), ALU.subtract).then_inc(c_lo, 1)

            def residual(b):
                if b == 0:
                    dve.wait_ge(tg_ready, 1)
                dve.wait_ge(o_ps, b + 1)
                x4 = xs(b).rearrange("p (a t) d -> p a (t d)", a=2)
                nc.vector.scalar_tensor_tensor(out=x4, in0=pG[:], scalar=tg[:, 0:1], in1=x4,
                                               op0=ALU.mult, op1=ALU.add).then_inc(x1_ready, 1)

            def stats2(b):
                dve.wait_ge(x1_ready, b + 1)
                if b >= 1:
                    dve.wait_ge(rstd2, b)
                stats(1, xs(b), var2)

            def norm2(b):
                if b >= 1:
                    dve.wait_ge(s_zd[b - 1], 16)
                    dve.wait_ge(z2T_ps, b)
                else:
                    dve.wait_ge(bst_used, 2)
                normalise(1, b, xs(b), z2_sb, rstd2, z2_ready)

            def take_logits(b):
                dve.wait_ge(lg_ps, b + 1)
                nc.vector.tensor_copy(lg[:, b * BLK:(b + 1) * BLK, :].rearrange("p t e -> p (t e)"),
                                      pL[b][:, 0, 0:BLK * E]).then_inc(lg_ready, 1)

            dve.wait_ge(s_x[0], 16)
            stats(0, xs(0), var1)
            norm1(0)
            dve.wait_ge(s_bias, 16)
            for h in range(2):
                dve.wait_ge(k_ps, h + 1)
                last = nc.vector.tensor_scalar(kT[:, h, :], pS[:, h, 0:2 * KV], bcol[:, 2 + h:3 + h],
                                               DH ** -0.5, ALU.add, ALU.mult)
            link(last)
            link(nc.vector.tensor_copy(kT_hi[:].bitcast(F32R), kT[:]))
            nc.vector.tensor_tensor(kT_lo[:], kT[:], kT_hi[:], ALU.subtract).then_inc(kt_ready, 1)
            dve.wait_ge(s_cst, 16)
            for h in range(2):
                nc.vector.tensor_tensor(
                    kb_hi[:, 0, h, :].rearrange("p (h n) -> p h n", n=KV),
                    kT_hi[:, h, 0:KV].unsqueeze(1).broadcast_to([P, HH, KV]),
                    c("mask_k").unsqueeze(2).broadcast_to([P, HH, KV]), ALU.mult).then_inc(kh_ready, 1)
            mask_v = c("mask_v").rearrange("p (k h) -> p k h", h=HH)
            vb5 = vb[:].rearrange("p b a k (h w) -> p b a k h w", w=VW)

            def take_v(n):
                b, k = n // CH, n % CH
                dve.wait_ge(v_ps, n + 1)
                for h in range(2):
                    last = nc.vector.tensor_tensor(
                        vb5[0:CLEN[k], b, h, k, :, 0:DH],
                        pV[0:CLEN[k], n % 2, h * P:(h + 1) * P].rearrange("p (h w) -> p h w", w=DH),
                        mask_v[0:CLEN[k], k, :].unsqueeze(2).broadcast_to([CLEN[k], HH, DH]), ALU.mult)
                last.then_inc(v_ready, 1)

            split_z(0)
            take_v(0)
            take_v(1)
            split_q(0, 0)
            take_v(2)
            split_q(0, 1)
            for i in range(2 * BLK):
                reduce_max(0, i // BLK, i % BLK)
                if i + 3 < BATCH * CH:
                    take_v(i + 3)
                if i == 4:
                    dve.wait_ge(s_x[1], 16)
                    stats(0, xs(1), var1)
            norm1(1)
            for b in range(BATCH):
                for h in range(2):
                    last = nc.vector.tensor_copy(vb5[:, b, h, :, :, DH], mask_v)
            last.then_inc(v_ready, 1)
            nc.vector.memset(tri16[:, 1, :], 1.0)
            dve.wait_ge(wo_h, 1)
            nc.vector.tensor_tensor(wo_lo[:].rearrange("p k n -> p (k n)"), stage[:, 1, :],
                                    wo_hi[:].rearrange("p k n -> p (k n)").bitcast(F32),
                                    ALU.subtract).then_inc(wo_ready, 1)
            dve.wait_ge(bo_ps, 1)
            dve.wait_ge(s_brow, 32)
            link(nc.vector.tensor_tensor(brow[0:1, :], pV[0:1, 0, 0:D], brow[0:1, :], ALU.add))
            dve.wait_ge(m_zero, 1)
            link(nc.vector.tensor_copy(obias[0:1, :], brow[0:1, :]))
            nc.vector.tensor_tensor(obias[32:33, :], brow[0:1, :], obias[0:1, :].bitcast(F32),
                                    ALU.subtract).then_inc(ob_ready, 1)

            def over_e(t):
                return t.unsqueeze(2).broadcast_to([P, HT, E])

            e8 = c("iota_e8").unsqueeze(1).broadcast_to([P, HT, E])

            def softmax_start(n):
                dve.wait_ge(lg_ready, 2 * (n + 1))
                logit = lg[:, n * HT:(n + 1) * HT, :]
                link(nc.vector.tensor_reduce(red1[:], logit, AX_X, ALU.max))
                nc.vector.tensor_tensor(pr[:], logit, over_e(red1[:]), ALU.subtract).then_inc(dif_ready, 1)

            def softmax_end(n):
                dve.wait_ge(e_ready, n + 1)
                link(nc.vector.tensor_reduce(red1[:], tmp[:], AX_X, ALU.add))
                link(nc.vector.reciprocal(red2[:], red1[:]))
                link(nc.vector.tensor_tensor(pr[:], tmp[:], over_e(red2[:]), ALU.mult))

            def choose(n, k):
                hot, top = (m1, m2)[k], ptop[:, k, n * HT:(n + 1) * HT]
                link(nc.vector.tensor_reduce(top, pr[:], AX_X, ALU.max))
                link(nc.vector.tensor_tensor(tmp[:], pr[:], over_e(top), ALU.is_equal))
                link(nc.vector.tensor_tensor(tmp[:], tmp[:], e8, ALU.mult))
                link(nc.vector.tensor_reduce(red1[:], tmp[:], AX_X, ALU.min))
                link(nc.vector.tensor_tensor(hot[:], e8, over_e(red1[:]), ALU.is_equal))
                if k == 0:
                    link(nc.vector.scalar_tensor_tensor(out=pr[:], in0=hot[:], scalar=-2.0, in1=pr[:],
                                                        op0=ALU.mult, op1=ALU.add))
                else:
                    nc.vector.tensor_tensor(m16[:], m1[:], m2[:], ALU.add).then_inc(m_done, 1)

            def count(n):
                dve.wait_ge(rank_ps, n + 1)
                link(nc.vector.tensor_copy(cnt[:], pR[n][:, 1, 0:HT * E].rearrange("p (t e) -> p e t", e=E)))
                link(nc.vector.tensor_tensor_scan(inc[:].rearrange("p e t -> p (e t)"), c("not_first"),
                                                  cnt[:].rearrange("p e t -> p (e t)"), 0.0, ALU.mult, ALU.add))
                nc.vector.tensor_tensor(base[:], inc[:], cnt[:], ALU.subtract)
                link(nc.vector.tensor_scalar(nt_i[:], inc[:, :, HT - 1], float(P - 1), None, ALU.add))
                link(nc.vector.tensor_scalar(nt_s[:], nt_i[:], 7, None, ALU.logical_shift_right))
                link(nc.vector.tensor_copy(nt[:], nt_s[:]))
                link(nc.vector.tensor_tensor_scan(ends[:], c("ones_e"), nt[:], 0.0, ALU.mult, ALU.add))
                link(nc.vector.tensor_tensor(starts[:], ends[:], nt[:], ALU.subtract))

            def place_pairs(n):
                link(nc.vector.scalar_tensor_tensor(out=base[:], in0=starts[:].unsqueeze(2).broadcast_to([P, E, HT]),
                                                    scalar=float(P), in1=base[:], op0=ALU.mult, op1=ALU.add))
                link(nc.vector.tensor_tensor(pos3[:], pR[n][:, 0, 0:HT * E].rearrange("p (t e) -> p t e", e=E),
                                             base[:].rearrange("p e t -> p t e"), ALU.add))
                for k, hot in enumerate((m1, m2)):
                    last = nc.vector.tensor_tensor(seli[:, k, :, :], pos3[:], hot[:], ALU.mult)
                link(last)
                link(nc.vector.tensor_reduce(pos[:], seli[:].rearrange("p k t e -> p (k t) e"), AX_X, ALU.add))
                link(nc.vector.tensor_copy(pos_i[:], pos[:]))
                nc.vector.tensor_scalar(pa_i[:], pos_i[:], 7, None, ALU.logical_shift_right)
                link(nc.vector.tensor_scalar(pb_i[:], pos_i[:], P - 1, None, ALU.bitwise_and))
                nc.vector.tensor_copy(pa[:], pa_i[:])
                link(nc.vector.tensor_copy(pb[:], pb_i[:]))

            def one_hots(n):
                link(nc.vector.tensor_tensor(hot_a[:], c("iota_t").unsqueeze(1).broadcast_to([P, Q, NT]),
                                             pa[:].unsqueeze(2).broadcast_to([P, Q, NT]), ALU.is_equal))
                for k in range(TOPK):
                    sl = slice(k * HT, (k + 1) * HT)
                    nc.vector.tensor_tensor(val_a[:, sl, :], hot_a[:, sl, :],
                                            c("tok1").unsqueeze(2).broadcast_to([P, HT, NT]), ALU.mult)
                for g in range(2):
                    sl = slice(g * HT, (g + 1) * HT)
                    nc.vector.tensor_tensor(hot_b[:, sl, :], c("iota_p").unsqueeze(1).broadcast_to([P, HT, P]),
                                            pb[:, sl].unsqueeze(2).broadcast_to([P, HT, P]),
                                            ALU.is_equal).then_inc(hot_ready, 1)

            def experts(n):
                link(nc.vector.tensor_tensor(le[:], c("iota_t")[0:1, :].unsqueeze(2).broadcast_to([1, NT, E]),
                                             ends[0:1, :].unsqueeze(1).broadcast_to([1, NT, E]), ALU.is_ge))
                link(nc.vector.tensor_reduce(ex_f[:], le[:], AX_X, ALU.add))
                nc.vector.tensor_scalar(ex_i[:, n * NT:(n + 1) * NT], ex_f[:], float(E - 1), None,
                                        ALU.min).then_inc(ex_ready, 1)

            def list_slots(n):
                sl = slice(n * NT, (n + 1) * NT)
                dve.wait_ge(tab_ps, n + 1)
                link(nc.vector.tensor_copy(tab[:, 0:2, :].rearrange("p a n -> p (a n)"), pR[n][:, 0, 0:2 * NT]))
                nc.vector.tensor_scalar(tab[:, 3, :], tab[:, 1, :], 0.0, float(SEQ), ALU.is_gt, ALU.mult)
                link(nc.vector.tensor_tensor(tab[:, 2, :], tab[:, 0, :], tab[:, 1, :], ALU.add))
                nc.vector.tensor_scalar(src_i[:, sl], tab[:, 2, :], -1.0, 0.0, ALU.add, ALU.max)
                link(nc.vector.scalar_tensor_tensor(out=tab[:, 4, :], in0=tab[:, 2, :], scalar=0.0, in1=c("idle"),
                                                    op0=ALU.is_equal, op1=ALU.mult))
                link(nc.vector.tensor_tensor(tab[:, 3, :], tab[:, 3, :], tab[:, 4, :], ALU.add))
                nc.vector.scalar_tensor_tensor(out=dst_i[:, sl], in0=tab[:, 2, :], scalar=-1.0, in1=tab[:, 3, :],
                                               op0=ALU.add, op1=ALU.add).then_inc(idx_ready, 1)

            for b in range(BLOCKS):
                nxt, prev = b + 1 < BLOCKS, b >= 1
                if nxt:
                    split_z(b + 1)
                if prev:
                    normalise_attention(b - 1, 1)
                if b >= 2:
                    take_logits(b - 2)
                if b == BLOCKS - 1:
                    softmax_start(0)
                    softmax_end(0)
                    choose(0, 0)
                    choose(0, 1)
                    count(0)
                    place_pairs(0)
                if nxt:
                    split_q(b + 1, 0)
                    for i in range(3):
                        reduce_max(b + 1, 0, i)
                    split_q(b + 1, 1)
                    reduce_max(b + 1, 0, 3)
                if b + 2 < BLOCKS:
                    dve.wait_ge(s_x[b + 2], 16)
                    stats(0, xs(b + 2), var1)
                if prev:
                    split_c(b - 1)
                if b == BLOCKS - 1:
                    one_hots(0)
                    experts(0)
                    list_slots(0)
                if nxt:
                    reduce_max(b + 1, 1, 0)
                if b + 2 < BLOCKS:
                    norm1(b + 2)
                if nxt:
                    for i in range(1, BLK):
                        reduce_max(b + 1, 1, i)
                if prev:
                    residual(b - 1)
                    stats2(b - 1)
                normalise_attention(b, 0)
                if prev:
                    norm2(b - 1)
            normalise_attention(BLOCKS - 1, 1)

            def x_low(j):
                dve.wait_ge(x_hi, j + 1)
                nc.vector.tensor_tensor(xT_lo[:, j % 2, :], pS[:, 0, 0:D], xT_hi[:, j % 2, :].bitcast(F32),
                                        ALU.subtract).then_inc(x_lo, 1)

            def h_low(j):
                dve.wait_ge(h_hi, j + 1)
                nc.vector.tensor_tensor(hT_lo[:, j % 2, :], pS[:, 1, 0:D], hT_hi[:, j % 2, :].bitcast(F32),
                                        ALU.subtract).then_inc(h_lo, 1)

            def take_y(j):
                dve.wait_ge(y_ps, j + 1)
                if j >= YRING:
                    dve.wait_ge(s_ys[j % YRING], 16 * (j // YRING))
                nc.vector.tensor_copy(y_sb[:, j % YRING, :], pV[:, j % 2, 0:D]).then_inc(y_ready, 1)

            def combine(t):
                b = t // BLK
                if t % BLK == 0:
                    dve.wait_ge(s_yc[b], 16 * TOPK)
                for k in range(TOPK):
                    last = nc.vector.scalar_tensor_tensor(
                        out=x_sb[:, t, :], in0=yc[k][:, t, :], scalar=ptop[:, k, t:t + 1],
                        in1=x_sb[:, t, :], op0=ALU.mult, op1=ALU.add)
                    if k == 0:
                        link(last)
                if t % BLK == BLK - 1:
                    last.then_inc(out_ready, 1)

            def scale_top(n):
                top = ptop[:, :, n * HT:(n + 1) * HT]
                link(nc.vector.tensor_scalar(top, top, tg[:, 1:2], None, ALU.mult))

            x_low(0)
            x_low(1)
            for j in range(ALL + 2):
                if 1 <= j <= ALL:
                    h_low(j - 1)
                if j >= 2:
                    take_y(j - 2)
                if j + 2 < ALL:
                    x_low(j + 2)
                if j == 1:
                    take_logits(2)
                elif j == 2:
                    split_c(3)
                elif j == 4:
                    residual(3)
                elif j == 5:
                    stats2(3)
                elif j == 6:
                    norm2(3)
                elif j == 8:
                    take_logits(3)
                    softmax_start(1)
                elif j == 9:
                    softmax_end(1)
                elif j == 10:
                    choose(1, 0)
                elif j == 11:
                    choose(1, 1)
                elif j == 12:
                    count(1)
                elif j == 13:
                    place_pairs(1)
                elif j == 14:
                    one_hots(1)
                elif j == 16:
                    experts(1)
                    list_slots(1)
                elif j == NT + 6:
                    scale_top(0)
                elif NT + 7 <= j < NT + 7 + HT:
                    combine(j - NT - 7)
            scale_top(1)
            for t in range(HT, TILES):
                combine(t)

        @block.tensor
        def _(pe):
            def product(out, pairs, extra=None):
                for n, (l, r) in enumerate(pairs):
                    last = nc.tensor.matmul(out, l, r, start=(n == 0), stop=(n == len(pairs) - 1))
                return last

            pe.wait_ge(s_ctx, 16)
            pe.wait_ge(s_wk, 16)
            for h in range(2):
                product(pS[:, h, 0:2 * KV], [(wk_sb[:, k, h * P:(h + 1) * P], ctxT[:, k, :])
                                             for k in range(2)]).then_inc(k_ps, 1)

            def transpose_z(b):
                pe.wait_ge(z_ready, b + 1)
                if b == 0:
                    pe.wait_ge(s_cst, 16)
                if b >= 1:
                    pe.wait_ge(q_lo, 2 * b)
                if b >= 3:
                    pe.wait_ge(x1_ready, b - 2)
                for k in range(2):
                    for i in range(BLK):
                        last = nc.tensor.transpose(pG[:, k, i * P:(i + 1) * P],
                                                   z_sb[:, i, k * P:(k + 1) * P], ident)
                    last.then_inc(zT_ps, 1)

            def make_q(b, h):
                pe.wait_ge(z_lo, 2 * b + 2)
                if b == 0:
                    pe.wait_ge(wq_ready, 1)
                cols = slice(h * P, (h + 1) * P)
                product(pG[:, h, :], [(w[:, k, cols], z[:, k, :]) for k in range(2) for w, z in
                                      ((wq_hi, zq_hi), (wq_hi, zq_lo), (wq_lo, zq_hi))]).then_inc(q_ps, 1)

            def head_scores(b, h, i):
                n = 8 * b + 4 * h + i
                if i == 0:
                    pe.wait_ge(q_hi, 2 * b + h + 1)
                    if b < 2:
                        pe.wait_ge(kh_ready, 2)
                    else:
                        pe.wait_ge(k1_ready, 4)
                if b >= 1 and h == 0 and i == 0:
                    pe.wait_ge(m_ready, b)
                if b >= 3 and h == 0 and i == 0:
                    pe.wait_ge(lg_ready, b - 2)
                for g in range(2):
                    if n >= 1:
                        pe.wait_ge(sm_red, 2 * n + g - 1)
                    nc.tensor.matmul(pM[:, g, 0:4 * KV], qT_hi[:, unit(b, h), i * P:(i + 1) * P],
                                     kb_hi[:, b // 2, h, g * 4 * KV:(g + 1) * 4 * KV],
                                     start=True, stop=True).then_inc(sm_ps, 1)

            def transpose_max(b):
                pe.wait_ge(sm_red, 16 * (b + 1))
                for i in range(BLK):
                    last = nc.tensor.transpose(pM[0:NH, 0, i * P:(i + 1) * P], mx[:, i, :], ident)
                last.then_inc(mT_ps, 1)

            def scores(b, s):
                h, k = s // CH, s % CH
                n = 2 * CH * b + s
                if k == 0:
                    pe.wait_ge(q_lo, 2 * b + h + 1)
                if s == 0:
                    pe.wait_ge(m_ready, b + 1)
                if n == 0:
                    pe.wait_ge(cst_ready, 1)
                    pe.wait_ge(kl_ready, 2)
                if n >= 2:
                    pe.wait_ge(exp_done, n - 1)
                rows = slice(k * CS, k * CS + CLEN[k])
                u, kb = unit(b, h), b // 2
                product(pS[0:CLEN[k], n % 2, :],
                        [(kb_hi[:, kb, h, rows], qT_hi[:, u, :]), (kb_hi[:, kb, h, rows], qT_lo[:, u, :]),
                         (kb_lo[:, kb, h, rows], qT_hi[:, u, :]),
                         (sel[:, h, rows], m_sb[:, b % 2, :])]).then_inc(s_ps, 1)

            def weigh(b, h, i):
                n = 2 * b + h
                if i == 0:
                    pe.wait_ge(exp_done, 2 * CH * b + CH * (h + 1))
                    if n == 0:
                        pe.wait_ge(v_ready, BATCH * CH + 1)
                        pe.wait_ge(ob_ready, 1)
                    else:
                        pe.wait_ge(normed, n)
                off = (i % 2) * 256
                product(pV[:, i // 2, off:off + HH * VW],
                        [(prob[0:CLEN[k], (h * CH + k) * BN + i * P:(h * CH + k) * BN + (i + 1) * P],
                          vb[0:CLEN[k], b // 2, h, k, :]) for k in range(CH)]).then_inc(pv_ps, 1)

            def transpose_c(b):
                pe.wait_ge(normed, 2 * (b + 1))
                if b == 3:
                    pe.wait_ge(lg_ready, 3)
                pe.wait_ge(q_lo, min(2 * (b + 3), 2 * BLOCKS))
                for k in range(2):
                    for i in range(BLK):
                        last = nc.tensor.transpose(pG[:, k, i * P:(i + 1) * P],
                                                   c_sb[:, i, k * P:(k + 1) * P], ident)
                last.then_inc(cT_ps, 1)

            def project(b):
                pe.wait_ge(c_lo, b + 1)
                if b == 0:
                    pe.wait_ge(ob_ready, 1)
                for i in range(BLK):
                    t = slice(i * P, (i + 1) * P)
                    last = product(pG[:, i // 2, (i % 2) * D:(i % 2 + 1) * D],
                                   [(z[:, k, t], w[:, k, :]) for k in range(2) for z, w in
                                    ((zq_hi, wo_hi), (zq_hi, wo_lo), (zq_lo, wo_hi))]
                                   + [(ones_a[:], obias[:])])
                last.then_inc(o_ps, 1)

            def transpose_z2(b):
                pe.wait_ge(z2_ready, b + 1)
                if b < 2:
                    pe.wait_ge(m_ready, b + 3)
                for k in range(2):
                    for i in range(BLK):
                        last = nc.tensor.transpose(pL[b][:, k, i * P:(i + 1) * P],
                                                   z2_sb[:, i, k * P:(k + 1) * P], ident)
                last.then_inc(z2T_ps, 1)

            def logits(b):
                pe.wait_ge(z2T_ready, b + 1)
                if b == 0:
                    pe.wait_ge(s_rw, 16)
                for i in range(BLK):
                    last = product(pL[b][:, 0, i * E:(i + 1) * E],
                                   [(z2T[:, k, i * P:(i + 1) * P], rw[:, k, :]) for k in range(2)])
                last.then_inc(lg_ps, 1)

            def ranks(n):
                pe.wait_ge(m_done, n + 1)
                m = m16[:].rearrange("p t e -> p (t e)")
                nc.tensor.matmul(pR[n][:, 0, 0:HT * E], tri16[:, 0, :], m, start=True, stop=True)
                nc.tensor.matmul(pR[n][:, 1, 0:HT * E], tri16[:, 1, :], m, start=True,
                                 stop=True).then_inc(rank_ps, 1)

            def slot_list(n):
                for k in range(TOPK):
                    pe.wait_ge(hot_ready, TOPK * n + k + 1)
                    for t in range(HT):
                        last = nc.tensor.matmul(pR[n][:, 0, k * NT:(k + 1) * NT], hot_b[:, k * HT + t, :],
                                                val_a[:, k * HT + t, :], start=(t == 0), stop=(t == HT - 1))
                last.then_inc(tab_ps, 1)

            zq_hi, zq_lo = zT_hi, zT_lo
            def make_v(n):
                b, k = n // CH, n % CH
                if n == 0:
                    pe.wait_ge(rep_ready, 1)
                    pe.wait_ge(s_wv, 16)
                if n >= 2:
                    pe.wait_ge(v_ready, n - 1)
                product(pV[0:CLEN[k], n % 2, 0:D],
                        [(ctx_rep[:, kk, b, k * CS:k * CS + CLEN[k]], wv_sb[:, kk, :])
                         for kk in range(2)]).then_inc(v_ps, 1)

            transpose_z(0)
            make_v(0)
            make_v(1)
            make_q(0, 0)
            make_v(2)
            make_q(0, 1)
            for i in range(2 * BLK):
                head_scores(0, i // BLK, i % BLK)
                if i + 3 < BATCH * CH:
                    make_v(i + 3)
            transpose_max(0)
            pe.wait_ge(v_ready, BATCH * CH)
            pe.wait_ge(s_wo, 16)
            pe.wait_ge(s_bias, 16)
            product(pV[0:1, 0, 0:D], [(bcol[:, 4 + k:5 + k], stage[:, 1, k * D:(k + 1) * D])
                                      for k in range(2)]).then_inc(bo_ps, 1)
            for b in range(BLOCKS):
                nxt, prev = b + 1 < BLOCKS, b >= 1
                for s in range(2 * CH):
                    if nxt and s == 9:
                        head_scores(b + 1, 1, 3)
                    scores(b, s)
                    if prev and s in (0, 1):
                        weigh(b - 1, 1, 2 * s)
                        weigh(b - 1, 1, 2 * s + 1)
                    if nxt and s == 0:
                        transpose_z(b + 1)
                    if b >= 2 and s == 1:
                        transpose_z2(b - 2)
                    if nxt and s == 2:
                        make_q(b + 1, 0)
                    if b >= 2 and s == 2:
                        logits(b - 2)
                    if nxt and 3 <= s <= 8:
                        head_scores(b + 1, (s - 3) // 4, (s - 3) % 4)
                    if nxt and s == 5:
                        make_q(b + 1, 1)
                    if prev and s == 6:
                        transpose_c(b - 1)
                    if b == BLOCKS - 1 and s == 5:
                        ranks(0)
                    if b == BLOCKS - 1 and s == 8:
                        slot_list(0)
                    if prev and s == 8:
                        project(b - 1)
                    if nxt and s == 8:
                        head_scores(b + 1, 1, 2)
                    if nxt and s == 9:
                        transpose_max(b + 1)
                    if s >= 6:
                        weigh(b, 0, s - 6)
            for i in range(BLK):
                weigh(BLOCKS - 1, 1, i)

            def transpose_x(j):
                pe.wait_ge(s_xg[j % XRING], 16 * (j // XRING + 1))
                if j >= 1:
                    pe.wait_ge(x_lo, j)
                else:
                    pe.wait_ge(exp_done, 2 * CH * BLOCKS)
                for k in range(2):
                    last = nc.tensor.transpose(pS[:, 0, k * P:(k + 1) * P],
                                               xg[:, j % XRING, k * P:(k + 1) * P], ident)
                last.then_inc(xT_ps, 1)

            def layer(out, hi, lo, w, e, ones):
                pairs = [(ones[:], btab[:, bass.ds(e * D, D)])]
                for k in range(2):
                    w_h = w_hi[w][:, bass.ds(e * 2 * D + k * D, D)]
                    w_l = w_lo[w][:, bass.ds(e * 2 * D + k * D, D)]
                    cols = slice(k * P, (k + 1) * P)
                    pairs += [(hi[:, cols], w_h), (lo[:, cols], w_h), (hi[:, cols], w_l)]
                return product(out, pairs)

            def first(j, e):
                pe.wait_ge(x_lo, j + 1)
                if j == 0:
                    pe.wait_ge(idx_ready, 1)
                if j >= 2:
                    pe.wait_ge(h_ready, j - 1)
                layer(pM[:, j % 2, 0:D], xT_hi[:, j % 2, :], xT_lo[:, j % 2, :], 0, e,
                      ones_a).then_inc(h_ps, 1)

            def transpose_h(j):
                pe.wait_ge(h_ready, j + 1)
                if j >= 1:
                    pe.wait_ge(h_lo, j)
                for k in range(2):
                    last = nc.tensor.transpose(pS[:, 1, k * P:(k + 1) * P],
                                               h_sb[:, j % 2, k * P:(k + 1) * P], ident)
                last.then_inc(hT_ps, 1)

            def second(j, e):
                pe.wait_ge(h_lo, j + 1)
                if j >= 2:
                    pe.wait_ge(y_ready, j - 1)
                if j == 0:
                    pe.wait_ge(normed, 2 * BLOCKS)
                layer(pV[:, j % 2, 0:D], hT_hi[:, j % 2, :], hT_lo[:, j % 2, :], 1, e,
                      ones_b).then_inc(y_ps, 1)

            pe.wait_ge(stage_used, 2 * E)
            pe.wait_ge(bst_used, 2)
            expert = {}
            transpose_x(0)
            transpose_x(1)
            for j in range(ALL + 2):
                if j < ALL:
                    if j % NT == 0:
                        pe.wait_ge(ex_ready, j // NT + 1)
                    expert[j] = nc.tensor.value_load(ex_i[0:1, j:j + 1], min_val=0, max_val=E - 1)
                    first(j, expert[j])
                if 1 <= j <= ALL:
                    transpose_h(j - 1)
                if j >= 2:
                    second(j - 2, expert[j - 2])
                if j + 2 < ALL:
                    transpose_x(j + 2)
                if j == 0:
                    transpose_z2(2)
                elif j == 1:
                    logits(2)
                elif j == 2:
                    transpose_c(3)
                elif j == 4:
                    project(3)
                elif j == 7:
                    transpose_z2(3)
                elif j == 8:
                    logits(3)
                elif j == 12:
                    ranks(1)
                elif j == 15:
                    slot_list(1)


def kernel(**inputs):
    import concourse.bacc as _bacc
    from concourse.bass_utils import run_bass_kernel_spmd as _run

    def rows(name, *shape):
        return np.ascontiguousarray(np.asarray(inputs[name]).reshape(shape))

    def turned(name):
        return np.ascontiguousarray(np.asarray(inputs[name]).T)

    const, place = constants()
    g = [np.asarray(inputs[n]).reshape(1, 1) for n in ("g_xattn", "g_ffn")]
    arrays = {
        "x": rows("x", TOK, D),
        "ctx_t": np.ascontiguousarray(np.asarray(inputs["ctx_1024"]).reshape(BATCH * KV, D).T),
        "wq_t": turned("L0_xattn_Wq"), "wk_t": turned("L0_xattn_Wk"),
        "wv_t": turned("L0_xattn_Wv"), "wo_t": turned("L0_xattn_Wo"),
        "bcol": np.ascontiguousarray(np.concatenate(
            [np.asarray(inputs[f"L0_xattn_b{n}"]).reshape(2, P) for n in "qkv"]).T),
        "bo": rows("L0_xattn_bo", 1, D),
        "gates": np.ascontiguousarray(np.tile(np.concatenate(g, 1), (P, 1))),
        "router": rows("L0_ffn_router_w", D, E),
        "w_in": rows("L0_ffn_w_in", E, D, D), "w_out": rows("L0_ffn_w_out", E, D, D),
        "b_in": rows("L0_ffn_b_in", 1, E * D), "b_out": rows("L0_ffn_b_out", 1, E * D),
        "const": const,
    }
    nc = _bacc.Bacc("TRN2", target_bir_lowering=False, num_devices=1)
    aps = {n: nc.dram_tensor(f"in_{n}", v.shape, mybir.dt.from_np(v.dtype), kind="ExternalInput").ap()
           for n, v in arrays.items()}
    aps["out"] = nc.dram_tensor("out_0", (TOK, D), F32, kind="ExternalOutput").ap()
    build(nc, aps, place)
    r = _run(nc, [{f"in_{n}": v for n, v in arrays.items()}], core_ids=[0])
    return r.results[0]["out_0"].reshape(BATCH, SEQ, D)
```

```python
from contextlib import ExitStack

import numpy as np

import concourse.bass as bass
from concourse import mybir

F32 = mybir.dt.float32
F32R = mybir.dt.float32r
F16 = mybir.dt.float16
I32 = mybir.dt.int32
U32 = mybir.dt.uint32
ALU = mybir.AluOpType
ACT = mybir.ActivationFunctionType
AX_X = mybir.AxisListType.X

P = 128
BATCH, SEQ, D = 2, 1024, 256
KV, NH, DH = 77, 16, 16
E, TOPK = 8, 2
TOK = BATCH * SEQ
TILES = TOK // P
BLK = 4
BLOCKS = TILES // BLK
BN = BLK * P
HH = NH // 2
HALF = HH * KV
CH = 5
CS = HALF // CH
CLEN = [CS] * (CH - 1) + [HALF - CS * (CH - 1)]
CHEADS = [(CS * k // KV, (CS * k + CLEN[k] - 1) // KV + 1) for k in range(CH)]
MROW = 32
VW = DH + 1
HT = TILES // BATCH
PAIRS = SEQ * TOPK
NT = (PAIRS - E) // P + E
ALL = BATCH * NT
Q = TOPK * HT
PACK = 8
WORDS = -(-NT // PACK)
XRING = 8
YRING = 4
EPS = 1e-5
AFTER = {
    "project": 1, "z2T_2": 3, "logits_2": 4, "z2T_3": 6, "logits_3": 7, "ranks": 12,
    "slot_list": 17,
    "exp": 8,
    "norm2_2": 1, "residual": 2, "stats2": 3, "take_2": 4, "norm2_3": 5, "softmax_start": 7,
    "softmax_end": 8, "choose_0": 9, "choose_1": 10, "count": 12, "place": 13, "hot_tiles": 14,
    "hot_0": 14, "hot_1": 15, "experts": 16, "list": 17,
    "inv_std": 1,
}


def constants():
    p = np.arange(P)
    parts = {
        "ident": np.eye(P),
        "tri": (p[:, None] < p[None, :]),
        "mask_k": (p[:, None] // DH == np.arange(HH)[None, :]),
        "mask_v": np.stack([(CS * k + p)[:, None] // KV == np.arange(HH) for k in range(CH)], 1),
        "iota_p": np.broadcast_to(p, (P, P)),
        "iota_t": np.broadcast_to(np.arange(NT), (P, NT)),
        "iota_e8": np.broadcast_to(np.arange(E) - E, (P, E)),
        "not_first": np.broadcast_to(np.arange(E * HT) % HT != 0, (P, E * HT)),
        "ones_e": np.ones((P, E)),
        "bits": np.broadcast_to(float(E) ** (np.arange(WORDS * PACK) % PACK), (P, WORDS * PACK)),
        "tok1": p[:, None] + P * np.arange(HT)[None, :] + 1,
        "idle": PAIRS + 1 + p[:, None] + P * np.arange(NT)[None, :],
        "ones_a": np.broadcast_to(((p == 0) | (p == 32))[:, None], (P, P)),
        "ones_b": np.broadcast_to(((p == 64) | (p == 96))[:, None], (P, P)),
        "sel": p[:, None] % MROW == np.arange(HALF) // KV,
    }
    place, cols, at = {}, [], 0
    for name, a in parts.items():
        a = np.asarray(a, np.float32).reshape(P, -1)
        place[name] = (at, at + a.shape[1])
        at += a.shape[1]
        cols.append(a)
    return np.ascontiguousarray(np.concatenate(cols, 1)), place


def build(nc, a, place):
    ctx = ExitStack()
    with ctx:
        early, late = ExitStack(), ExitStack()

        def sb(name, shape, dt, st=ctx):
            return st.enter_context(nc.sbuf_tensor(name, shape, dt))

        def sem(name):
            return ctx.enter_context(nc.semaphore(name))

        n_small = place["sel"][0]
        x_sb = sb("x_sb", [P, TILES, D], F32)
        cst = sb("cst", [P, n_small], F32)
        gates_in = sb("gates_in", [P, 2], F32)
        tg = sb("tg", [P, 2], F32)
        w_hi = [sb(f"w{n}_hi", [P, E * 2 * D], F32R) for n in ("in", "out")]
        w_lo = [sb(f"w{n}_lo", [P, E * 2 * D], F32R) for n in ("in", "out")]
        btab = sb("btab", [P, E * D], F32R)
        ones_a = sb("ones_a", [P, P], F32R)
        ones_b = sb("ones_b", [P, P], F32R)
        tri16 = sb("tri16", [P, 2, P], F16)
        lg = sb("lg", [P, TILES, E], F32)

        zT_hi = sb("zT_hi", [P, 2, BN], F32R)
        zT_lo = sb("zT_lo", [P, 2, BN], F32R)
        c_sb = sb("c_sb", [P, BLK, D], F32)
        wo_hi = sb("wo_hi", [P, 2, D], F32R)
        wo_lo = sb("wo_lo", [P, 2, D], F32R)
        obias = sb("obias", [P, D], F32R)
        stage = sb("stage", [P, 2, 2 * D], F32)
        bcol = sb("bcol", [P, 6], F32)
        brow = sb("brow", [1, D], F32)
        mx = sb("mx", [P, BLK, MROW + HH], F32)
        st6 = sb("st6", [P, 2, BLK, 6], F32)
        mv = sb("mv", [P, 2, BLK, 2], F32)
        rstd = sb("rstd", [P, 2, BLK], F32)
        veps = sb("veps", [P, 2, BLK], F32)
        half = sb("half", [P, BLK], F32)
        rden = sb("rden", [P, BLK, HH], F32)
        z2T = sb("z2T", [P, 2, BN], F32)
        rw = sb("rw", [P, 2, E], F32)
        z2_sb = sb("z2_sb", [P, BLK, D], F32)
        ptop = sb("ptop", [P, TOPK, TILES], F32)
        src_i = sb("src_i", [P, ALL], U32)
        dst_i = sb("dst_i", [P, ALL], U32)
        ex_i = sb("ex_i", [1, BATCH * WORDS], I32)

        wq_hi = sb("wq_hi", [P, 2, D], F32R, early)
        wq_lo = sb("wq_lo", [P, 2, D], F32R, early)
        z_sb = sb("z_sb", [P, BLK, D], F32, early)
        kT = sb("kT", [P, 2, 2 * KV], F32, early)
        kT_hi = sb("kT_hi", [P, 2, 2 * KV], F32, early)
        kT_lo = sb("kT_lo", [P, 2, 2 * KV], F32, early)
        kb_hi = sb("kb_hi", [P, BATCH, 2, HALF], F32R, early)
        kb_lo = sb("kb_lo", [P, BATCH, 2, HALF], F32R, early)
        sel = sb("sel", [P, HALF], F32R, early)
        qT_hi = sb("qT_hi", [P, 3, BN], F32R, early)
        qT_lo = sb("qT_lo", [P, 3, BN], F32R, early)
        m_sb = sb("m_sb", [P, 2, BN], F32R, early)
        vb = sb("vb", [P, BATCH, 2, CH, HH * VW], F32, early)
        prob = sb("prob", [P, 2 * CH * BN], F32, early)
        at = [0]

        def setup_view(n):
            at[0] += n
            return prob[:, at[0] - n:at[0]]

        ctxT = setup_view(2 * 2 * KV).rearrange("p (k n) -> p k n", k=2)
        ctx_rep = setup_view(2 * 2 * HALF).rearrange("p (k b n) -> p k b n", k=2, b=2)
        wk_sb = setup_view(2 * D).rearrange("p (k n) -> p k n", k=2)
        wv_sb = setup_view(2 * D).rearrange("p (k n) -> p k n", k=2)
        sel_f = setup_view(HALF)
        early.close()

        def mo(name, shape, dt):
            return sb(name, shape, dt, late)

        pr = mo("pr", [P, HT, E], F32)
        tmp = mo("tmp", [P, HT, E], F32)
        m1 = mo("m1", [P, HT, E], F32)
        m2 = mo("m2", [P, HT, E], F32)
        m16 = mo("m16", [P, HT, E], F16)
        red1 = mo("red1", [P, HT], F32)
        red2 = mo("red2", [P, HT], F32)
        cnt = mo("cnt", [P, E, HT], F32)
        inc = mo("inc", [P, E, HT], F32)
        base = mo("base", [P, E, HT], F32)
        pos3 = mo("pos3", [P, HT, E], F32)
        seli = mo("seli", [P, TOPK, HT, E], F32)
        pos = mo("pos", [P, Q], F32)
        pos_i = mo("pos_i", [P, Q], I32)
        pa_i = mo("pa_i", [P, Q], I32)
        pb_i = mo("pb_i", [P, Q], I32)
        pa = mo("pa", [P, Q], F32)
        pb = mo("pb", [P, Q], F32)
        nt_i = mo("nt_i", [P, E], I32)
        nt_s = mo("nt_s", [P, E], I32)
        nt = mo("nt", [P, E], F32)
        ends = mo("ends", [P, E], F32)
        starts = mo("starts", [P, E], F32)
        le = mo("le", [1, WORDS * PACK, E], F32)
        word = mo("word", [1, WORDS], F32)
        ex_f = mo("ex_f", [1, WORDS * PACK], F32)
        hot_b = mo("hot_b", [P, Q, P], F16)
        hot_a = mo("hot_a", [P, Q, NT], F32)
        val_a = mo("val_a", [P, Q, NT], F16)
        tab = mo("tab", [P, 5, NT], F32)
        xg = mo("xg", [P, XRING, D], F32)
        xT_hi = mo("xT_hi", [P, 2, D], F32R)
        xT_lo = mo("xT_lo", [P, 2, D], F32R)
        h_sb = mo("h_sb", [P, 2, D], F32)
        hT_hi = mo("hT_hi", [P, 2, D], F32R)
        hT_lo = mo("hT_lo", [P, 2, D], F32R)
        y_sb = mo("y_sb", [P, YRING, D], F32)
        yc = [mo(f"yc{k}", [P, TILES, D], F32) for k in range(TOPK)]
        late.close()

        def pair(name):
            return ctx.enter_context(nc.psum_tensor(name, [P, 2, 512], F32))

        pG = pair("pG")
        pM = pair("pM")
        pS = pair("pS")
        pV = pair("pV")
        pL = [pM, pM, pG, pG]
        pR = [pM, pG]

        z_dram = [nc.dram_tensor(f"z_dram{n}", [SEQ, D], F32, kind="Internal").ap() for n in range(BATCH)]
        y_dram = [nc.dram_tensor(f"y_dram{n}", [PAIRS + NT * P, D], F32, kind="Internal").ap()
                  for n in range(BATCH)]

        s_x = [sem(f"s_x{b}") for b in range(BLOCKS)]
        s_ctx, s_wk, s_wv, s_cst, s_sel = sem("s_ctx"), sem("s_wk"), sem("s_wv"), sem("s_cst"), sem("s_sel")
        s_wq, s_wo, s_bias, s_brow, s_rw = sem("s_wq"), sem("s_wo"), sem("s_bias"), sem("s_brow"), sem("s_rw")
        s_stage = [sem("s_stage0"), sem("s_stage1")]
        s_bst = [sem("s_bst0"), sem("s_bst1")]
        s_zd = [sem(f"s_zd{b}") for b in range(BLOCKS)]
        s_xg = [sem(f"s_xg{r}") for r in range(XRING)]
        s_ys = [sem(f"s_ys{r}") for r in range(YRING)]
        s_yc = [sem(f"s_yc{t}") for t in range(TILES // 2)]
        s_out = sem("s_out")
        dve_step, pool_step, act_step = sem("dve_step"), sem("pool_step"), sem("act_step")
        rep_ready, wq_h, wo_h, tg_ready = sem("rep_ready"), sem("wq_h"), sem("wo_h"), sem("tg_ready")
        wq_ready, wo_ready = sem("wq_ready"), sem("wo_ready")
        k_ps, kt_ready, v_ps, v_raw, v_ready, warm_ready = sem("k_ps"), sem("kt_ready"), sem("v_ps"), sem("v_raw"), sem("v_ready"), sem("warm_ready")
        kh_ready, kl_ready, k1_ready, ones_ready = sem("kh_ready"), sem("kl_ready"), sem("k1_ready"), sem("ones_ready")
        bo_ps, ob_ready, cst_ready, m_zero = sem("bo_ps"), sem("ob_ready"), sem("cst_ready"), sem("m_zero")
        bst_zero, bst_used, btab_ready, stage_used = sem("bst_zero"), sem("bst_used"), sem("btab_ready"), sem("stage_used")
        var1, var2, rstd1, rstd2 = sem("var1"), sem("var2"), sem("rstd1"), sem("rstd2")
        z_ready, zT_ps, z_hi, z_lo = sem("z_ready"), sem("zT_ps"), sem("z_hi"), sem("z_lo")
        q_ps, q_hi, q_lo = sem("q_ps"), sem("q_hi"), sem("q_lo")
        sm_ps, sm_red, mT_ps, m_ready = sem("sm_ps"), sem("sm_red"), sem("mT_ps"), sem("m_ready")
        s_ps, exp_done, pv_ps, normed = sem("s_ps"), sem("exp_done"), sem("pv_ps"), sem("normed")
        cT_ps, c_hi, c_lo, o_ps = sem("cT_ps"), sem("c_hi"), sem("c_lo"), sem("o_ps")
        x1_ready, z2_ready, z2T_ps, z2T_ready = sem("x1_ready"), sem("z2_ready"), sem("z2T_ps"), sem("z2T_ready")
        lg_ps, lg_ready = sem("lg_ps"), sem("lg_ready")
        dif_ready, e_ready, m_done, rank_ps = sem("dif_ready"), sem("e_ready"), sem("m_done"), sem("rank_ps")
        hot_ready, tab_ps, ex_ready, idx_ready = sem("hot_ready"), sem("tab_ps"), sem("ex_ready"), sem("idx_ready")
        xT_ps, x_hi, x_lo = sem("xT_ps"), sem("x_hi"), sem("x_lo")
        h_ps, h_ready, hT_ps, h_hi, h_lo = sem("h_ps"), sem("h_ready"), sem("hT_ps"), sem("h_hi"), sem("h_lo")
        y_ps, y_ready, combined, out_ready = sem("y_ps"), sem("y_ready"), sem("combined"), sem("out_ready")

        def c(name):
            lo, hi = place[name]
            return cst[:, lo:hi]

        ident = c("ident")
        x_t = a["x"].rearrange("(b t p) d -> b p t d", p=P, t=BLK)
        out_t = a["out"].rearrange("(b t p) d -> b p t d", p=P, t=2)
        z_t = [z.rearrange("(b t p) d -> b p t d", p=P, t=BLK) for z in z_dram]
        y_t = [y[0:PAIRS, :].rearrange("(k b t p) d -> k b p t d", p=P, t=2, k=TOPK) for y in y_dram]

        def unit(blk, half):
            return (2 * blk + half) % 3

        block = ctx.enter_context(nc.Block())

        @block.sync
        def _(sp):
            def two(w):
                return w.rearrange("(k p) n -> p k n", p=P)

            sp.dma_start(x_sb[:, 0:BLK, :], x_t[0]).then_inc(s_x[0], 16)
            sp.dma_start(ctxT, two(a["ctx_t"])).then_inc(s_ctx, 16)
            sp.dma_start(wk_sb, two(a["wk_t"])).then_inc(s_wk, 16)
            sp.dma_start(cst[:], a["const"][:, 0:n_small]).then_inc(s_cst, 16)
            sp.dma_start(bcol[:], a["bcol"]).then_inc(s_bias, 16)
            sp.dma_start(stage[:, 0, :].rearrange("p (k n) -> p k n", k=2), two(a["wq_t"])).then_inc(s_wq, 16)
            sp.dma_start(wv_sb, two(a["wv_t"])).then_inc(s_wv, 16)
            sp.dma_start(sel_f, a["const"][:, n_small:]).then_inc(s_sel, 16)
            sp.dma_start(x_sb[:, BLK:2 * BLK, :], x_t[1]).then_inc(s_x[1], 16)
            sp.dma_start(stage[:, 1, :].rearrange("p (k n) -> p k n", k=2), two(a["wo_t"])).then_inc(s_wo, 16)
            sp.dma_start(brow[0:1, :], a["bo"]).then_inc(s_brow, 16)
            sp.dma_start(gates_in[:], a["gates"]).then_inc(s_brow, 16)
            sp.dma_start(rw[:], a["router"].rearrange("(k p) e -> p k e", p=P)).then_inc(s_rw, 16)
            for b in range(2, BLOCKS):
                sp.dma_start(x_sb[:, b * BLK:(b + 1) * BLK, :], x_t[b]).then_inc(s_x[b], 16)
            for g in range(2):
                sp.wait_ge(bst_zero, 1)
                if g:
                    sp.wait_ge(bst_used, 1)
                for row, name in ((0, "b_in"), (32, "b_in"), (64, "b_out"), (96, "b_out")):
                    sp.dma_start(z2_sb[row:row + 1, :, :].rearrange("p e d -> p (e d)"),
                                 a[name][:, g * BLK * D:(g + 1) * BLK * D]).then_inc(s_bst[g], 16)
            sp.wait_ge(wq_ready, 1)
            for u in range(2 * E):
                e, which = u // 2, u % 2
                if u == 1:
                    sp.wait_ge(wo_ready, 1)
                    sp.wait_ge(bo_ps, 1)
                if u >= 2:
                    sp.wait_ge(stage_used, u - 1)
                w = a["w_out" if which else "w_in"]
                sp.dma_start(stage[:, u % 2, :].rearrange("p (k n) -> p k n", k=2),
                             w[e].rearrange("(k p) n -> p k n", p=P)).then_inc(s_stage[u % 2], 16)
            for n in range(BATCH):
                for r in range(YRING):
                    sp.wait_ge(s_ys[r], 16 * len(range(r, (n + 1) * NT, YRING)))
                for u in range(n * HT // 2, (n + 1) * HT // 2):
                    for k in range(TOPK):
                        sp.dma_start(yc[k][:, 2 * u:2 * u + 2, :],
                                     y_t[n][k, u - n * HT // 2]).then_inc(s_yc[u], 16)
                for u in range(n * HT // 2, (n + 1) * HT // 2):
                    sp.wait_ge(out_ready, u + 1)
                    sp.dma_start(out_t[u], x_sb[:, 2 * u:2 * u + 2, :]).then_inc(s_out, 16)
            sp.wait_ge(s_out, 16 * TILES // 2)

        @block.gpsimd
        def _(pool):
            step = [0]

            def link(ins):
                step[0] += 1
                ins.then_inc(pool_step, 1)
                pool.wait_ge(pool_step, step[0])

            def inv_std(which, n, src, done):
                pool.wait_ge(src, n + 1)
                link(nc.gpsimd.tensor_scalar(veps[:, which, :], mv[:, which, :, 1], EPS, None, ALU.add))
                nc.gpsimd.tensor_tensor(rstd[:, which, :], veps[:, which, :], half[:],
                                        ALU.pow).then_inc(done, 1)

            def split_weights(u0, u1):
                for u in range(u0, u1):
                    e, which = u // 2, u % 2
                    sl = slice(e * 2 * D, (e + 1) * 2 * D)
                    pool.wait_ge(s_stage[u % 2], 16 * (u // 2 + 1))
                    link(nc.gpsimd.tensor_copy(w_hi[which][:, sl], stage[:, u % 2, :]))
                    nc.gpsimd.tensor_tensor(w_lo[which][:, sl], stage[:, u % 2, :],
                                            w_hi[which][:, sl].bitcast(F32),
                                            ALU.subtract).then_inc(stage_used, 1)

            nc.gpsimd.memset(z2_sb[:], 0.0).then_inc(bst_zero, 1)
            link(nc.gpsimd.memset(half[:], -0.5))
            nc.gpsimd.memset(obias[:].bitcast(F32), 0.0).then_inc(m_zero, 1)
            nc.gpsimd.memset(m_sb[:].bitcast(F32), 0.0).then_inc(m_zero, 1)
            nc.gpsimd.memset(mx[:], 0.0).then_inc(m_zero, 1)
            def key_blocks(b, part, dst, done):
                for h in range(2):
                    nc.gpsimd.tensor_tensor(
                        dst[:, b, h, :].rearrange("p (h n) -> p h n", n=KV),
                        part[:, h, b * KV:(b + 1) * KV].unsqueeze(1).broadcast_to([P, HH, KV]),
                        c("mask_k").unsqueeze(2).broadcast_to([P, HH, KV]), ALU.mult).then_inc(done, 1)

            inv_std(0, 0, var1, rstd1)
            link(nc.gpsimd.memset(vb[:], 0.0))
            pool.wait_ge(wq_h, 1)
            nc.gpsimd.tensor_tensor(wq_lo[:].rearrange("p k n -> p (k n)"), stage[:, 0, :],
                                    wq_hi[:].rearrange("p k n -> p (k n)").bitcast(F32),
                                    ALU.subtract).then_inc(wq_ready, 1)
            pool.wait_ge(s_cst, 16)
            pool.wait_ge(kt_ready, 1)
            key_blocks(0, kT_lo, kb_lo, kl_ready)
            mask_v = c("mask_v").rearrange("p (k h) -> p k h", h=HH)
            vb5 = vb[:].rearrange("p b a k (h w) -> p b a k h w", w=VW)
            for n in range(BATCH * CH):
                b, k = n // CH, n % CH
                pool.wait_ge(v_raw, n + 1)
                h0, h1 = CHEADS[k]
                nh = h1 - h0
                nc.gpsimd.tensor_tensor(
                    vb5[0:CLEN[k], b, :, k, h0:h1, 0:DH],
                    c_sb[0:CLEN[k], n % BLK, 0:2 * nh * DH].rearrange("p (a h w) -> p a h w", a=2, w=DH),
                    mask_v[0:CLEN[k], k, h0:h1].unsqueeze(1).unsqueeze(3).broadcast_to([CLEN[k], 2, nh, DH]),
                    ALU.mult).then_inc(v_ready, 1)
                if n == 3:
                    inv_std(0, 1, var1, rstd1)
            for b in range(BATCH):
                for h in range(2):
                    last = nc.gpsimd.tensor_copy(vb5[:, b, h, :, :, DH], mask_v)
            last.then_inc(v_ready, 1)
            key_blocks(1, kT_hi, kb_hi, k1_ready)
            key_blocks(1, kT_lo, kb_lo, k1_ready)
            for g in range(2):
                pool.wait_ge(s_bst[g], 64)
                sl = slice(g * BLK * D, (g + 1) * BLK * D)
                src = z2_sb[:].rearrange("p e d -> p (e d)")
                link(nc.gpsimd.tensor_copy(btab[:, sl], src))
                for row in (32, 96):
                    last = nc.gpsimd.tensor_tensor(btab[row:row + 1, sl], src[row:row + 1, :],
                                                   btab[row:row + 1, sl].bitcast(F32), ALU.subtract)
                    if row == 32:
                        link(last)
                last.then_inc(bst_used, 1)
                pool.wait_ge(bst_used, g + 1)
                if g == 0:
                    inv_std(0, 2, var1, rstd1)
            split_weights(0, 4)
            inv_std(0, 3, var1, rstd1)
            split_weights(4, 7)
            inv_std(1, 0, var2, rstd2)
            split_weights(7, 12)
            inv_std(1, 1, var2, rstd2)
            split_weights(12, 2 * E)

            def gather(j):
                r, n = j % XRING, j // NT
                if j % NT == 0:
                    for b in range(2 * n, 2 * n + 2):
                        pool.wait_ge(s_zd[b], 16)
                    pool.wait_ge(idx_ready, n + 1)
                if j >= XRING:
                    pool.wait_ge(xT_ps, j - XRING + 1)
                if j == 0:
                    pool.wait_ge(s_ps, 2 * CH * BLOCKS)
                pool.indirect_dma_start(
                    out=xg[:, r, :], out_offset=None, in_=z_dram[n],
                    in_offset=bass.IndirectOffsetOnAxis(ap=src_i[:, j:j + 1], axis=0),
                ).then_inc(s_xg[r], 16)

            def scatter(j):
                r = j % YRING
                pool.wait_ge(y_ready, j + 1)
                pool.indirect_dma_start(
                    out=y_dram[j // NT], out_offset=bass.IndirectOffsetOnAxis(ap=dst_i[:, j:j + 1], axis=0),
                    in_=y_sb[:, r, :], in_offset=None,
                ).then_inc(s_ys[r], 16)

            for j in range(XRING):
                gather(j)
                if j == 4:
                    inv_std(1, 2, var2, rstd2)
            for j in range(ALL):
                scatter(j)
                if j == AFTER["inv_std"]:
                    inv_std(1, 3, var2, rstd2)
                if j + XRING < ALL:
                    gather(j + XRING)

        @block.scalar
        def _(act):
            act.wait_ge(s_ctx, 16)
            for k in range(2):
                for b in range(BATCH):
                    last = nc.scalar.activation(
                        ctx_rep[:, k, b, :].rearrange("p (h n) -> p h n", h=HH),
                        ctxT[:, k, b * KV:(b + 1) * KV].unsqueeze(1).broadcast_to([P, HH, KV]), ACT.Copy)
            last.then_inc(rep_ready, 1)
            act.wait_ge(s_wq, 16)
            nc.scalar.activation(wq_hi[:].rearrange("p k n -> p (k n)"), stage[:, 0, :], ACT.Copy).then_inc(wq_h, 1)
            def split_z(b):
                act.wait_ge(zT_ps, 2 * b + 2)
                if b >= 3:
                    act.wait_ge(o_ps, b - 2)
                for k in range(2):
                    nc.scalar.activation(zT_hi[:, k, :], pG[:, k, :], ACT.Copy).then_inc(z_hi, 1)

            def split_q(b, h):
                act.wait_ge(q_ps, 2 * b + h + 1)
                if 2 * b + h >= 3:
                    act.wait_ge(s_ps, CH * (2 * b + h - 2))
                nc.scalar.activation(qT_hi[:, unit(b, h), :], pG[:, h, :], ACT.Identity,
                                     bias=bcol[:, h:h + 1]).then_inc(q_hi, 1)

            def negate_max(b, h):
                act.wait_ge(mT_ps, b + 2 if b else h + 1)
                rows = slice(MROW * h, MROW * h + HH)
                src = pG if b == 0 and h == 0 else pM
                nc.scalar.activation(m_sb[rows, h, :], src[rows, 0, :], ACT.Copy, scale=-1.0).then_inc(m_ready, 1)

            def exp(b, s):
                h, k = s // CH, s % CH
                n = 2 * CH * b + s
                act.wait_ge(s_ps, n + 1)
                if b >= 1 and k == 0:
                    act.wait_ge(pv_ps, BLK * (2 * (b - 1) + h + 1))
                nc.scalar.activation(prob[0:CLEN[k], s * BN:(s + 1) * BN], pS[0:CLEN[k], n % 2, :],
                                     ACT.Exp).then_inc(exp_done, 1)

            def split_c(b):
                act.wait_ge(cT_ps, b + 1)
                act.wait_ge(q_ps, min(2 * (b + 3), 2 * BLOCKS))
                nc.scalar.activation(zT_hi[:], pG[:], ACT.Copy).then_inc(c_hi, 1)

            def copy_z2(b):
                act.wait_ge(z2T_ps, b + 1)
                if b >= 1:
                    act.wait_ge(lg_ps, b)
                nc.scalar.activation(z2T[:], pL[b][:], ACT.Copy).then_inc(z2T_ready, 1)
                nc.scalar.dma_start(z_t[b // 2][b % 2], z2_sb[:]).then_inc(s_zd[b], 16)

            def router_exp(n):
                act.wait_ge(dif_ready, n + 1)
                nc.scalar.activation(tmp[:], pr[:], ACT.Exp).then_inc(e_ready, 1)

            def take_v(n):
                k = n % CH
                act.wait_ge(v_ps, n + 1)
                if n >= BLK:
                    act.wait_ge(v_ready, n - BLK + 1)
                width = 2 * (CHEADS[k][1] - CHEADS[k][0]) * DH
                nc.scalar.activation(c_sb[0:CLEN[k], n % BLK, 0:width], pV[0:CLEN[k], n % 2, 0:width],
                                     ACT.Copy).then_inc(v_raw, 1)

            act.wait_ge(s_bias, 16)
            for b in range(-1, BLOCKS):
                main = b >= 0
                nxt = b + 1 < BLOCKS
                prev = b >= 1
                for s in range(2 * CH):
                    if main:
                        if b == 0 and s == 0:
                            act.wait_ge(v_ps, BATCH * CH)
                            act.wait_ge(cst_ready, 1)
                        exp(b, s)
                    if s == 0 and nxt:
                        split_z(b + 1)
                    if s == 1 and b >= 2:
                        copy_z2(b - 2)
                    if s == 1 and b == -1:
                        for n in range(CH):
                            take_v(n)
                    if s == 2 and nxt:
                        split_q(b + 1, 0)
                    if s == 5 and nxt:
                        split_q(b + 1, 1)
                    if s == 5 and b == -1:
                        for n in range(CH, 2 * CH):
                            take_v(n)
                        act.wait_ge(s_sel, 16)
                        nc.scalar.activation(sel[:], sel_f, ACT.Copy).then_inc(cst_ready, 1)
                        act.wait_ge(m_zero, 2)
                        negate_max(0, 0)
                        nc.scalar.activation(tri16[:, 0, :], c("tri"), ACT.Copy)
                        nc.scalar.activation(ones_a[:], c("ones_a"), ACT.Copy)
                        nc.scalar.activation(ones_b[:], c("ones_b"), ACT.Copy).then_inc(ones_ready, 1)
                        act.wait_ge(s_wo, 16)
                        nc.scalar.activation(wo_hi[:].rearrange("p k n -> p (k n)"), stage[:, 1, :],
                                             ACT.Copy).then_inc(wo_h, 1)
                        act.wait_ge(s_brow, 32)
                        nc.scalar.activation(tg[:], gates_in[:], ACT.Tanh).then_inc(tg_ready, 1)
                    if s == 2 and b == BLOCKS - 1:
                        router_exp(0)
                    if s == (4 if b == BLOCKS - 1 else 6) and prev:
                        split_c(b - 1)
                    if b == 0 and s == 3:
                        negate_max(0, 1)
                if nxt and main:
                    negate_max(b + 1, 0)
                    negate_max(b + 1, 1)

            def x_high(j):
                act.wait_ge(xT_ps, j + 1)
                if j >= 2:
                    act.wait_ge(h_ps, j - 1)
                nc.scalar.activation(xT_hi[:, j % 2, :], pS[:, 0, 0:D], ACT.Copy).then_inc(x_hi, 1)

            def gelu(j):
                act.wait_ge(h_ps, j + 1)
                if j >= 2:
                    act.wait_ge(hT_ps, j - 1)
                nc.scalar.activation(h_sb[:, j % 2, :], pM[:, j % 2, 0:D],
                                     ACT.Gelu_apprx_tanh).then_inc(h_ready, 1)

            def h_high(j):
                act.wait_ge(hT_ps, j + 1)
                if j >= 2:
                    act.wait_ge(y_ps, j - 1)
                nc.scalar.activation(hT_hi[:, j % 2, :], pS[:, 1, 0:D], ACT.Copy).then_inc(h_hi, 1)

            def take_y(j):
                act.wait_ge(y_ps, j + 1)
                if j >= YRING:
                    act.wait_ge(s_ys[j % YRING], 16 * (j // YRING))
                nc.scalar.activation(y_sb[:, j % YRING, :], pV[:, j % 2, 0:D], ACT.Copy).then_inc(y_ready, 1)

            x_high(0)
            split_c(3)
            x_high(1)
            for j in range(ALL + 2):
                if j < ALL:
                    gelu(j)
                if 1 <= j <= ALL:
                    h_high(j - 1)
                if j >= 2:
                    take_y(j - 2)
                if j + 2 < ALL:
                    x_high(j + 2)
                if j == AFTER["z2T_2"]:
                    copy_z2(2)
                if j == AFTER["z2T_3"]:
                    copy_z2(3)
                if j == AFTER["exp"]:
                    router_exp(1)

        @block.vector
        def _(dve):
            step = [0]

            def link(ins):
                step[0] += 1
                ins.then_inc(dve_step, 1)
                dve.wait_ge(dve_step, step[0])

            def stats(which, src, done):
                for i in range(BLK):
                    last = nc.vector.bn_stats(st6[:, which, i, :], src[:, i, :])
                link(last)
                for i in range(BLK):
                    last = nc.vector.bn_aggr(mv[:, which, i, :], st6[:, which, i, :])
                last.then_inc(done, 1)

            def normalise(which, n, src, dst, inv, done):
                dve.wait_ge(inv, n + 1)
                for i in range(BLK):
                    last = nc.vector.tensor_scalar(dst[:, i, :], src[:, i, :], mv[:, which, i, 0:1],
                                                   rstd[:, which, i:i + 1], ALU.subtract, ALU.mult)
                last.then_inc(done, 1)

            def xs(b):
                return x_sb[:, b * BLK:(b + 1) * BLK, :]

            def norm1(b):
                if b >= 1:
                    dve.wait_ge(zT_ps, 2 * b)
                normalise(0, b, xs(b), z_sb, rstd1, z_ready)

            def split_z(b):
                for k in range(2):
                    dve.wait_ge(z_hi, 2 * b + k + 1)
                    nc.vector.tensor_tensor(zT_lo[:, k, :], pG[:, k, :], zT_hi[:, k, :].bitcast(F32),
                                            ALU.subtract).then_inc(z_lo, 1)

            def split_q(b, h):
                dve.wait_ge(q_hi, 2 * b + h + 1)
                u = unit(b, h)
                nc.vector.scalar_tensor_tensor(out=qT_lo[:, u, :], in0=pG[:, h, :], scalar=bcol[:, h:h + 1],
                                               in1=qT_hi[:, u, :].bitcast(F32), op0=ALU.add,
                                               op1=ALU.subtract).then_inc(q_lo, 1)

            def reduce_max(b, h, i):
                n = 8 * b + 4 * h + i
                if b >= 1 and n % 8 == 0:
                    dve.wait_ge(mT_ps, b + 1)
                if n == 0:
                    dve.wait_ge(m_zero, 3)
                for g in range(2):
                    dve.wait_ge(sm_ps, 2 * n + g + 1)
                    nc.vector.tensor_reduce(mx[:, i, MROW * h + 4 * g:MROW * h + 4 * g + 4],
                                            pM[:, g, 0:4 * KV].rearrange("p (h n) -> p h n", n=KV),
                                            AX_X, ALU.max).then_inc(sm_red, 1)

            def normalise_attention(b, h):
                n = 2 * b + h
                dve.wait_ge(pv_ps, BLK * (n + 1))
                v = pV[:].rearrange("p a (t w) -> p (a t) w", t=2)[:, :, 0:HH * VW].rearrange(
                    "p t (h w) -> p t h w", w=VW)
                link(nc.vector.reciprocal(rden[:], v[:, :, :, DH]))
                if b >= 1 and h == 0:
                    dve.wait_ge(cT_ps, b)
                if n == 0:
                    dve.wait_ge(v_ready, BATCH * CH)
                nc.vector.tensor_tensor(
                    c_sb[:, :, h * P:(h + 1) * P].rearrange("p t (h w) -> p t h w", w=DH),
                    v[:, :, :, 0:DH], rden[:].unsqueeze(3).broadcast_to([P, BLK, HH, DH]),
                    ALU.mult).then_inc(normed, 1)

            def split_c(b):
                dve.wait_ge(c_hi, b + 1)
                nc.vector.tensor_tensor(zT_lo[:], pG[:], zT_hi[:].bitcast(F32), ALU.subtract).then_inc(c_lo, 1)

            def residual(b):
                if b == 0:
                    dve.wait_ge(tg_ready, 1)
                dve.wait_ge(o_ps, b + 1)
                x4 = xs(b).rearrange("p (a t) d -> p a (t d)", a=2)
                nc.vector.scalar_tensor_tensor(out=x4, in0=pG[:], scalar=tg[:, 0:1], in1=x4,
                                               op0=ALU.mult, op1=ALU.add).then_inc(x1_ready, 1)

            def stats2(b):
                dve.wait_ge(x1_ready, b + 1)
                if b >= 1:
                    dve.wait_ge(rstd2, b)
                stats(1, xs(b), var2)

            def norm2(b):
                if b >= 1:
                    dve.wait_ge(s_zd[b - 1], 16)
                    dve.wait_ge(z2T_ps, b)
                else:
                    dve.wait_ge(bst_used, 2)
                normalise(1, b, xs(b), z2_sb, rstd2, z2_ready)

            def take_logits(b):
                dve.wait_ge(lg_ps, b + 1)
                nc.vector.tensor_copy(lg[:, b * BLK:(b + 1) * BLK, :].rearrange("p t e -> p (t e)"),
                                      pL[b][:, 0, 0:BLK * E]).then_inc(lg_ready, 1)

            nc.vector.memset(zT_hi[:, 0, :].bitcast(F32), 0.0).then_inc(warm_ready, 1)
            dve.wait_ge(s_x[0], 16)
            stats(0, xs(0), var1)
            norm1(0)
            dve.wait_ge(s_bias, 16)
            for h in range(2):
                dve.wait_ge(k_ps, h + 1)
                last = nc.vector.tensor_scalar(kT[:, h, :], pS[:, h, 0:2 * KV], bcol[:, 2 + h:3 + h],
                                               DH ** -0.5, ALU.add, ALU.mult)
            link(last)
            link(nc.vector.tensor_copy(kT_hi[:].bitcast(F32R), kT[:]))
            nc.vector.tensor_tensor(kT_lo[:], kT[:], kT_hi[:], ALU.subtract).then_inc(kt_ready, 1)
            dve.wait_ge(s_cst, 16)
            split_z(0)
            for h in range(2):
                nc.vector.tensor_tensor(
                    kb_hi[:, 0, h, :].rearrange("p (h n) -> p h n", n=KV),
                    kT_hi[:, h, 0:KV].unsqueeze(1).broadcast_to([P, HH, KV]),
                    c("mask_k").unsqueeze(2).broadcast_to([P, HH, KV]), ALU.mult).then_inc(kh_ready, 1)
            dve.wait_ge(s_x[1], 16)
            stats(0, xs(1), var1)
            split_q(0, 0)
            split_q(0, 1)
            for i in range(BLK):
                reduce_max(0, 0, i)
            norm1(1)
            def output_bias():
                nc.vector.memset(tri16[:, 1, :], 1.0)
                dve.wait_ge(wo_h, 1)
                nc.vector.tensor_tensor(wo_lo[:].rearrange("p k n -> p (k n)"), stage[:, 1, :],
                                        wo_hi[:].rearrange("p k n -> p (k n)").bitcast(F32),
                                        ALU.subtract).then_inc(wo_ready, 1)
                dve.wait_ge(bo_ps, 1)
                dve.wait_ge(s_brow, 32)
                link(nc.vector.tensor_tensor(brow[0:1, :], pV[0:1, 0, 0:D], brow[0:1, :], ALU.add))
                dve.wait_ge(m_zero, 1)
                link(nc.vector.tensor_copy(obias[0:1, :], brow[0:1, :]))
                nc.vector.tensor_tensor(obias[32:33, :], brow[0:1, :], obias[0:1, :].bitcast(F32),
                                        ALU.subtract).then_inc(ob_ready, 1)

            def over_e(t):
                return t.unsqueeze(2).broadcast_to([P, HT, E])

            e8 = c("iota_e8").unsqueeze(1).broadcast_to([P, HT, E])

            def softmax_start(n):
                dve.wait_ge(lg_ready, 2 * (n + 1))
                logit = lg[:, n * HT:(n + 1) * HT, :]
                link(nc.vector.tensor_reduce(red1[:], logit, AX_X, ALU.max))
                nc.vector.tensor_tensor(pr[:], logit, over_e(red1[:]), ALU.subtract).then_inc(dif_ready, 1)

            def softmax_end(n):
                dve.wait_ge(e_ready, n + 1)
                link(nc.vector.tensor_reduce(red1[:], tmp[:], AX_X, ALU.add))
                link(nc.vector.reciprocal(red2[:], red1[:]))
                link(nc.vector.tensor_tensor(pr[:], tmp[:], over_e(red2[:]), ALU.mult))

            def choose(n, k):
                hot, top = (m1, m2)[k], ptop[:, k, n * HT:(n + 1) * HT]
                link(nc.vector.tensor_reduce(top, pr[:], AX_X, ALU.max))
                link(nc.vector.tensor_tensor(tmp[:], pr[:], over_e(top), ALU.is_equal))
                link(nc.vector.tensor_tensor(tmp[:], tmp[:], e8, ALU.mult))
                link(nc.vector.tensor_reduce(red1[:], tmp[:], AX_X, ALU.min))
                link(nc.vector.tensor_tensor(hot[:], e8, over_e(red1[:]), ALU.is_equal))
                if k == 0:
                    link(nc.vector.scalar_tensor_tensor(out=pr[:], in0=hot[:], scalar=-2.0, in1=pr[:],
                                                        op0=ALU.mult, op1=ALU.add))
                else:
                    nc.vector.tensor_tensor(m16[:], m1[:], m2[:], ALU.add).then_inc(m_done, 1)

            def count(n):
                dve.wait_ge(rank_ps, n + 1)
                link(nc.vector.tensor_copy(cnt[:], pR[n][:, 1, 0:HT * E].rearrange("p (t e) -> p e t", e=E)))
                link(nc.vector.tensor_tensor_scan(inc[:].rearrange("p e t -> p (e t)"), c("not_first"),
                                                  cnt[:].rearrange("p e t -> p (e t)"), 0.0, ALU.mult, ALU.add))
                nc.vector.tensor_tensor(base[:], inc[:], cnt[:], ALU.subtract)
                link(nc.vector.tensor_scalar(nt_i[:], inc[:, :, HT - 1], float(P - 1), None, ALU.add))
                link(nc.vector.tensor_scalar(nt_s[:], nt_i[:], 7, None, ALU.logical_shift_right))
                link(nc.vector.tensor_copy(nt[:], nt_s[:]))
                link(nc.vector.tensor_tensor_scan(ends[:], c("ones_e"), nt[:], 0.0, ALU.mult, ALU.add))
                link(nc.vector.tensor_tensor(starts[:], ends[:], nt[:], ALU.subtract))

            def place_pairs(n):
                link(nc.vector.scalar_tensor_tensor(out=base[:], in0=starts[:].unsqueeze(2).broadcast_to([P, E, HT]),
                                                    scalar=float(P), in1=base[:], op0=ALU.mult, op1=ALU.add))
                link(nc.vector.tensor_tensor(pos3[:], pR[n][:, 0, 0:HT * E].rearrange("p (t e) -> p t e", e=E),
                                             base[:].rearrange("p e t -> p t e"), ALU.add))
                for k, hot in enumerate((m1, m2)):
                    last = nc.vector.tensor_tensor(seli[:, k, :, :], pos3[:], hot[:], ALU.mult)
                link(last)
                link(nc.vector.tensor_reduce(pos[:], seli[:].rearrange("p k t e -> p (k t) e"), AX_X, ALU.add))
                link(nc.vector.tensor_copy(pos_i[:], pos[:]))
                nc.vector.tensor_scalar(pa_i[:], pos_i[:], 7, None, ALU.logical_shift_right)
                link(nc.vector.tensor_scalar(pb_i[:], pos_i[:], P - 1, None, ALU.bitwise_and))
                nc.vector.tensor_copy(pa[:], pa_i[:])
                link(nc.vector.tensor_copy(pb[:], pb_i[:]))

            def hot_tiles(n):
                link(nc.vector.tensor_tensor(hot_a[:], c("iota_t").unsqueeze(1).broadcast_to([P, Q, NT]),
                                             pa[:].unsqueeze(2).broadcast_to([P, Q, NT]), ALU.is_equal))
                for k in range(TOPK):
                    sl = slice(k * HT, (k + 1) * HT)
                    nc.vector.tensor_tensor(val_a[:, sl, :], hot_a[:, sl, :],
                                            c("tok1").unsqueeze(2).broadcast_to([P, HT, NT]), ALU.mult)

            def hot_places(n, k):
                sl = slice(k * HT, (k + 1) * HT)
                nc.vector.tensor_tensor(hot_b[:, sl, :], c("iota_p").unsqueeze(1).broadcast_to([P, HT, P]),
                                        pb[:, sl].unsqueeze(2).broadcast_to([P, HT, P]),
                                        ALU.is_equal).then_inc(hot_ready, 1)

            def experts(n):
                count = WORDS * PACK
                link(nc.vector.tensor_tensor(le[:], c("iota_p")[0:1, 0:count].unsqueeze(2).broadcast_to([1, count, E]),
                                             ends[0:1, :].unsqueeze(1).broadcast_to([1, count, E]), ALU.is_ge))
                link(nc.vector.tensor_reduce(ex_f[:], le[:], AX_X, ALU.add))
                link(nc.vector.scalar_tensor_tensor(out=ex_f[:], in0=ex_f[:], scalar=float(E - 1),
                                                    in1=c("bits")[0:1, :], op0=ALU.min, op1=ALU.mult))
                link(nc.vector.tensor_reduce(word[:], ex_f[:].rearrange("p (a b) -> p a b", b=PACK), AX_X,
                                             ALU.add))
                nc.vector.tensor_copy(ex_i[:, n * WORDS:(n + 1) * WORDS], word[:]).then_inc(ex_ready, 1)

            def list_slots(n):
                sl = slice(n * NT, (n + 1) * NT)
                dve.wait_ge(tab_ps, n + 1)
                link(nc.vector.tensor_copy(tab[:, 0:2, :].rearrange("p a n -> p (a n)"), pR[n][:, 0, 0:2 * NT]))
                nc.vector.tensor_scalar(tab[:, 3, :], tab[:, 1, :], 0.0, float(SEQ), ALU.is_gt, ALU.mult)
                link(nc.vector.tensor_tensor(tab[:, 2, :], tab[:, 0, :], tab[:, 1, :], ALU.add))
                nc.vector.tensor_scalar(src_i[:, sl], tab[:, 2, :], -1.0, 0.0, ALU.add, ALU.max)
                link(nc.vector.scalar_tensor_tensor(out=tab[:, 4, :], in0=tab[:, 2, :], scalar=0.0, in1=c("idle"),
                                                    op0=ALU.is_equal, op1=ALU.mult))
                link(nc.vector.tensor_tensor(tab[:, 3, :], tab[:, 3, :], tab[:, 4, :], ALU.add))
                nc.vector.scalar_tensor_tensor(out=dst_i[:, sl], in0=tab[:, 2, :], scalar=-1.0, in1=tab[:, 3, :],
                                               op0=ALU.add, op1=ALU.add).then_inc(idx_ready, 1)

            for b in range(BLOCKS):
                nxt, prev = b + 1 < BLOCKS, b >= 1
                if b == 0:
                    reduce_max(0, 1, 0)
                    reduce_max(0, 1, 1)
                if nxt:
                    split_z(b + 1)
                if b == 0:
                    reduce_max(0, 1, 2)
                    reduce_max(0, 1, 3)
                    output_bias()
                if b == BLOCKS - 1:
                    take_logits(b - 2)
                    softmax_start(0)
                if prev:
                    normalise_attention(b - 1, 1)
                if b == BLOCKS - 2:
                    take_logits(b - 2)
                if nxt:
                    split_q(b + 1, 0)
                    for i in range(3):
                        reduce_max(b + 1, 0, i)
                    split_q(b + 1, 1)
                    reduce_max(b + 1, 0, 3)
                if b + 2 < BLOCKS:
                    dve.wait_ge(s_x[b + 2], 16)
                    stats(0, xs(b + 2), var1)
                if b == BLOCKS - 1:
                    softmax_end(0)
                    choose(0, 0)
                if prev:
                    split_c(b - 1)
                if b == BLOCKS - 1:
                    choose(0, 1)
                    count(0)
                    place_pairs(0)
                    hot_tiles(0)
                    hot_places(0, 0)
                    hot_places(0, 1)
                if nxt:
                    for i in range(BLK):
                        reduce_max(b + 1, 1, i)
                if b + 2 < BLOCKS:
                    norm1(b + 2)
                if b == BLOCKS - 1:
                    normalise_attention(b, 0)
                    list_slots(0)
                    experts(0)
                if prev:
                    residual(b - 1)
                    stats2(b - 1)
                if nxt:
                    normalise_attention(b, 0)
                if prev and nxt:
                    norm2(b - 1)
            normalise_attention(BLOCKS - 1, 1)

            def x_low(j):
                dve.wait_ge(x_hi, j + 1)
                nc.vector.tensor_tensor(xT_lo[:, j % 2, :], pS[:, 0, 0:D], xT_hi[:, j % 2, :].bitcast(F32),
                                        ALU.subtract).then_inc(x_lo, 1)

            def h_low(j):
                dve.wait_ge(h_hi, j + 1)
                nc.vector.tensor_tensor(hT_lo[:, j % 2, :], pS[:, 1, 0:D], hT_hi[:, j % 2, :].bitcast(F32),
                                        ALU.subtract).then_inc(h_lo, 1)

            def combine(u, k):
                if k == 0:
                    dve.wait_ge(s_yc[u], 16 * TOPK)
                else:
                    dve.wait_ge(combined, u + 1)
                for t in (2 * u, 2 * u + 1):
                    last = nc.vector.scalar_tensor_tensor(
                        out=x_sb[:, t, :], in0=yc[k][:, t, :], scalar=ptop[:, k, t:t + 1],
                        in1=x_sb[:, t, :], op0=ALU.mult, op1=ALU.add)
                last.then_inc((combined, out_ready)[k], 1)

            def scale_top(n):
                top = ptop[:, :, n * HT:(n + 1) * HT]
                link(nc.vector.tensor_scalar(top, top, tg[:, 1:2], None, ALU.mult))

            x_low(0)
            split_c(3)
            x_low(1)
            for j in range(ALL + 2):
                if 1 <= j <= ALL:
                    h_low(j - 1)
                if j + 2 < ALL:
                    x_low(j + 2)
                if j == AFTER["norm2_2"]:
                    norm2(2)
                if j == AFTER["residual"]:
                    residual(3)
                if j == AFTER["stats2"]:
                    stats2(3)
                if j == AFTER["take_2"]:
                    take_logits(2)
                if j == AFTER["norm2_3"]:
                    norm2(3)
                if j == AFTER["softmax_start"]:
                    take_logits(3)
                    softmax_start(1)
                if j == AFTER["softmax_end"]:
                    softmax_end(1)
                if j == AFTER["choose_0"]:
                    choose(1, 0)
                if j == AFTER["choose_1"]:
                    choose(1, 1)
                if j == AFTER["count"]:
                    count(1)
                if j == AFTER["place"]:
                    place_pairs(1)
                if j == AFTER["hot_tiles"]:
                    hot_tiles(1)
                if j == AFTER["hot_0"]:
                    hot_places(1, 0)
                if j == AFTER["hot_1"]:
                    hot_places(1, 1)
                if j == AFTER["list"]:
                    list_slots(1)
                if j == AFTER["experts"]:
                    experts(1)
                if j == NT + 7:
                    scale_top(0)
                elif NT + 8 <= j < NT + 8 + HT:
                    combine((j - NT - 8) // 2, (j - NT - 8) % 2)
            scale_top(1)
            for u in range(HT // 2, TILES // 2):
                combine(u, 0)
                combine(u, 1)

        @block.tensor
        def _(pe):
            def product(out, pairs, extra=None):
                for n, (l, r) in enumerate(pairs):
                    last = nc.tensor.matmul(out, l, r, start=(n == 0), stop=(n == len(pairs) - 1))
                return last

            pe.wait_ge(warm_ready, 1)
            for _ in range(10):
                nc.tensor.matmul(pG[:, 0, :], zT_hi[:, 0, 0:P], zT_hi[:, 0, :], start=True, stop=True)

            pe.wait_ge(s_ctx, 16)
            pe.wait_ge(s_wk, 16)
            for h in range(2):
                product(pS[:, h, 0:2 * KV], [(wk_sb[:, k, h * P:(h + 1) * P], ctxT[:, k, :])
                                             for k in range(2)]).then_inc(k_ps, 1)

            def transpose_z(b):
                pe.wait_ge(z_ready, b + 1)
                if b == 0:
                    pe.wait_ge(s_cst, 16)
                if b >= 1:
                    pe.wait_ge(q_lo, 2 * b)
                if b >= 3:
                    pe.wait_ge(x1_ready, b - 2)
                for k in range(2):
                    for i in range(BLK):
                        last = nc.tensor.transpose(pG[:, k, i * P:(i + 1) * P],
                                                   z_sb[:, i, k * P:(k + 1) * P], ident)
                    last.then_inc(zT_ps, 1)

            def make_q(b, h):
                pe.wait_ge(z_lo, 2 * b + 2)
                if b == 0:
                    pe.wait_ge(wq_ready, 1)
                cols = slice(h * P, (h + 1) * P)
                product(pG[:, h, :], [(w[:, k, cols], z[:, k, :]) for k in range(2) for w, z in
                                      ((wq_hi, zq_hi), (wq_hi, zq_lo), (wq_lo, zq_hi))]).then_inc(q_ps, 1)

            def head_scores(b, h, i):
                n = 8 * b + 4 * h + i
                if i == 0:
                    pe.wait_ge(q_hi, 2 * b + h + 1)
                    if b < 2:
                        pe.wait_ge(kh_ready, 2)
                    else:
                        pe.wait_ge(k1_ready, 4)
                if b >= 1 and h == 0 and i == 0:
                    pe.wait_ge(m_ready, 2 * b)
                if b >= 3 and h == 0 and i == 0:
                    pe.wait_ge(lg_ready, b - 2)
                for g in range(2):
                    if n >= 1:
                        pe.wait_ge(sm_red, 2 * n + g - 1)
                    nc.tensor.matmul(pM[:, g, 0:4 * KV], qT_hi[:, unit(b, h), i * P:(i + 1) * P],
                                     kb_hi[:, b // 2, h, g * 4 * KV:(g + 1) * 4 * KV],
                                     start=True, stop=True).then_inc(sm_ps, 1)

            def transpose_max(b):
                pe.wait_ge(sm_red, 16 * (b + 1))
                for i in range(BLK):
                    last = nc.tensor.transpose(pM[0:MROW + HH, 0, i * P:(i + 1) * P], mx[:, i, :], ident)
                last.then_inc(mT_ps, 1)

            def transpose_first_max():
                pe.wait_ge(sm_red, 8)
                pe.wait_ge(q_lo, 2)
                for i in range(BLK):
                    last = nc.tensor.transpose(pG[0:HH, 0, i * P:(i + 1) * P], mx[:, i, 0:HH], ident)
                last.then_inc(mT_ps, 1)

            def scores(b, s):
                h, k = s // CH, s % CH
                n = 2 * CH * b + s
                if k == 0:
                    pe.wait_ge(q_lo, 2 * b + h + 1)
                if k == 0:
                    pe.wait_ge(m_ready, 2 * b + h + 1)
                if n == 0:
                    pe.wait_ge(cst_ready, 1)
                    pe.wait_ge(kl_ready, 2)
                if n >= 2:
                    pe.wait_ge(exp_done, n - 1)
                rows = slice(k * CS, k * CS + CLEN[k])
                u, kb = unit(b, h), b // 2
                product(pS[0:CLEN[k], n % 2, :],
                        [(kb_hi[:, kb, h, rows], qT_hi[:, u, :]), (kb_hi[:, kb, h, rows], qT_lo[:, u, :]),
                         (kb_lo[:, kb, h, rows], qT_hi[:, u, :]),
                         (sel[:, rows], m_sb[:, h, :])]).then_inc(s_ps, 1)

            def weigh(b, h, i):
                n = 2 * b + h
                if i == 0:
                    pe.wait_ge(exp_done, 2 * CH * b + CH * (h + 1))
                    if n == 0:
                        pe.wait_ge(v_ready, BATCH * CH + 1)
                        pe.wait_ge(ob_ready, 1)
                    else:
                        pe.wait_ge(normed, n)
                off = (i % 2) * 256
                product(pV[:, i // 2, off:off + HH * VW],
                        [(prob[0:CLEN[k], (h * CH + k) * BN + i * P:(h * CH + k) * BN + (i + 1) * P],
                          vb[0:CLEN[k], b // 2, h, k, :]) for k in range(CH)]).then_inc(pv_ps, 1)

            def transpose_c(b):
                pe.wait_ge(normed, 2 * (b + 1))
                if b >= 1:
                    pe.wait_ge(x1_ready, b)
                pe.wait_ge(q_lo, min(2 * (b + 3), 2 * BLOCKS))
                for k in range(2):
                    for i in range(BLK):
                        last = nc.tensor.transpose(pG[:, k, i * P:(i + 1) * P],
                                                   c_sb[:, i, k * P:(k + 1) * P], ident)
                last.then_inc(cT_ps, 1)

            def project(b):
                pe.wait_ge(c_lo, b + 1)
                if b == 0:
                    pe.wait_ge(ob_ready, 1)
                    pe.wait_ge(ones_ready, 1)
                for i in range(BLK):
                    t = slice(i * P, (i + 1) * P)
                    last = product(pG[:, i // 2, (i % 2) * D:(i % 2 + 1) * D],
                                   [(z[:, k, t], w[:, k, :]) for k in range(2) for z, w in
                                    ((zq_hi, wo_hi), (zq_hi, wo_lo), (zq_lo, wo_hi))]
                                   + [(ones_a[:], obias[:])])
                last.then_inc(o_ps, 1)

            def transpose_z2(b):
                pe.wait_ge(z2_ready, b + 1)
                if b < 2:
                    pe.wait_ge(m_ready, 2 * (b + 3))
                elif b == 2:
                    pe.wait_ge(x1_ready, 4)
                else:
                    pe.wait_ge(lg_ready, 3)
                for k in range(2):
                    for i in range(BLK):
                        last = nc.tensor.transpose(pL[b][:, k, i * P:(i + 1) * P],
                                                   z2_sb[:, i, k * P:(k + 1) * P], ident)
                last.then_inc(z2T_ps, 1)

            def logits(b):
                pe.wait_ge(z2T_ready, b + 1)
                if b == 0:
                    pe.wait_ge(s_rw, 16)
                for i in range(BLK):
                    last = product(pL[b][:, 0, i * E:(i + 1) * E],
                                   [(z2T[:, k, i * P:(i + 1) * P], rw[:, k, :]) for k in range(2)])
                last.then_inc(lg_ps, 1)

            def ranks(n):
                pe.wait_ge(m_done, n + 1)
                m = m16[:].rearrange("p t e -> p (t e)")
                nc.tensor.matmul(pR[n][:, 0, 0:HT * E], tri16[:, 0, :], m, start=True, stop=True)
                nc.tensor.matmul(pR[n][:, 1, 0:HT * E], tri16[:, 1, :], m, start=True,
                                 stop=True).then_inc(rank_ps, 1)

            def slot_list(n):
                for k in range(TOPK):
                    pe.wait_ge(hot_ready, TOPK * n + k + 1)
                    for t in range(HT):
                        last = nc.tensor.matmul(pR[n][:, 0, k * NT:(k + 1) * NT], hot_b[:, k * HT + t, :],
                                                val_a[:, k * HT + t, :], start=(t == 0), stop=(t == HT - 1))
                last.then_inc(tab_ps, 1)

            zq_hi, zq_lo = zT_hi, zT_lo
            def make_v(n):
                b, k = n // CH, n % CH
                if n == 0:
                    pe.wait_ge(rep_ready, 1)
                    pe.wait_ge(s_wv, 16)
                if n >= 2:
                    pe.wait_ge(v_raw, n - 1)
                h0, h1 = CHEADS[k]
                product(pV[0:CLEN[k], n % 2, 0:2 * (h1 - h0) * DH].rearrange("p (a v) -> p a v", a=2),
                        [(ctx_rep[:, kk, b, k * CS:k * CS + CLEN[k]],
                          wv_sb[:, kk, :].rearrange("p (a v) -> p a v", a=2)[:, :, h0 * DH:h1 * DH])
                         for kk in range(2)]).then_inc(v_ps, 1)

            transpose_z(0)
            for n in range(CH):
                make_v(n)
            make_q(0, 0)
            make_q(0, 1)
            for i in range(BLK):
                head_scores(0, 0, i)
                make_v(i + CH)
            make_v(2 * CH - 1)
            transpose_first_max()
            pe.wait_ge(v_raw, BATCH * CH)
            pe.wait_ge(s_wo, 16)
            pe.wait_ge(s_bias, 16)
            product(pV[0:1, 0, 0:D], [(bcol[:, 4 + k:5 + k], stage[:, 1, k * D:(k + 1) * D])
                                      for k in range(2)]).then_inc(bo_ps, 1)
            for b in range(BLOCKS):
                nxt, prev = b + 1 < BLOCKS, b >= 1
                for s in range(2 * CH):
                    if nxt and s == 9:
                        head_scores(b + 1, 1, 3)
                    scores(b, s)
                    if b == 0 and s in (0, 1):
                        head_scores(0, 1, s)
                    if b == 0 and s == 2:
                        head_scores(0, 1, 2)
                        head_scores(0, 1, 3)
                    if b == 0 and s == 3:
                        transpose_max(0)
                    late = b == BLOCKS - 1
                    if nxt and s == 0:
                        transpose_z(b + 1)
                    if prev and s in (1, 2):
                        weigh(b - 1, 1, 2 * s - 2)
                        if late and s == 2:
                            logits(b - 2)
                        weigh(b - 1, 1, 2 * s - 1)
                    if b >= 2 and s == 1:
                        transpose_z2(b - 2)
                    if nxt and s == 2:
                        make_q(b + 1, 0)
                    if b == BLOCKS - 2 and s == 2:
                        logits(b - 2)
                    if late and s == 4:
                        transpose_c(b - 1)
                    if late and s == 7:
                        project(b - 1)
                    if nxt and 3 <= s <= 8:
                        head_scores(b + 1, (s - 3) // 4, (s - 3) % 4)
                    if nxt and s == 5:
                        make_q(b + 1, 1)
                    if prev and not late and s == 8:
                        project(b - 1)
                    if nxt and s == 8:
                        head_scores(b + 1, 1, 2)
                    if nxt and s == 9:
                        transpose_max(b + 1)
                    if s >= 6:
                        weigh(b, 0, s - 6)
                    if prev and not late and s == 6:
                        transpose_c(b - 1)
                    if late and s == 6:
                        ranks(0)
                    if late and s == 9:
                        slot_list(0)
            for i in range(BLK):
                weigh(BLOCKS - 1, 1, i)

            def transpose_x(j):
                pe.wait_ge(s_xg[j % XRING], 16 * (j // XRING + 1))
                if j >= 1:
                    pe.wait_ge(x_lo, j)
                else:
                    pe.wait_ge(exp_done, 2 * CH * BLOCKS)
                for k in range(2):
                    last = nc.tensor.transpose(pS[:, 0, k * P:(k + 1) * P],
                                               xg[:, j % XRING, k * P:(k + 1) * P], ident)
                last.then_inc(xT_ps, 1)

            def layer(out, hi, lo, w, e, ones):
                pairs = [(ones[:], btab[:, bass.ds(e * D, D)])]
                for k in range(2):
                    w_h = w_hi[w][:, bass.ds(e * 2 * D + k * D, D)]
                    w_l = w_lo[w][:, bass.ds(e * 2 * D + k * D, D)]
                    cols = slice(k * P, (k + 1) * P)
                    pairs += [(hi[:, cols], w_h), (lo[:, cols], w_h), (hi[:, cols], w_l)]
                return product(out, pairs)

            def first(j, e):
                pe.wait_ge(x_lo, j + 1)
                if j == 0:
                    pe.wait_ge(idx_ready, 1)
                if j >= 2:
                    pe.wait_ge(h_ready, j - 1)
                layer(pM[:, j % 2, 0:D], xT_hi[:, j % 2, :], xT_lo[:, j % 2, :], 0, e,
                      ones_a).then_inc(h_ps, 1)

            def transpose_h(j):
                pe.wait_ge(h_ready, j + 1)
                if j >= 1:
                    pe.wait_ge(h_lo, j)
                for k in range(2):
                    last = nc.tensor.transpose(pS[:, 1, k * P:(k + 1) * P],
                                               h_sb[:, j % 2, k * P:(k + 1) * P], ident)
                last.then_inc(hT_ps, 1)

            def second(j, e):
                pe.wait_ge(h_lo, j + 1)
                if j >= 2:
                    pe.wait_ge(y_ready, j - 1)
                if j == 0:
                    pe.wait_ge(normed, 2 * BLOCKS)
                layer(pV[:, j % 2, 0:D], hT_hi[:, j % 2, :], hT_lo[:, j % 2, :], 1, e,
                      ones_b).then_inc(y_ps, 1)

            pe.wait_ge(stage_used, 2 * E)
            pe.wait_ge(bst_used, 2)
            expert = {}
            transpose_x(0)
            transpose_c(3)
            transpose_x(1)
            for j in range(ALL + 2):
                if j < ALL:
                    n, l = j // NT, j % NT
                    if l == 0:
                        pe.wait_ge(ex_ready, n + 1)
                    if l % PACK == 0:
                        packed = nc.tensor.value_load(ex_i[0:1, n * WORDS + l // PACK:n * WORDS + l // PACK + 1],
                                                    min_val=0, max_val=E ** PACK - 1)
                    expert[j] = (packed >> (3 * (l % PACK))) & (E - 1)
                    first(j, expert[j])
                if 1 <= j <= ALL:
                    transpose_h(j - 1)
                if j >= 2:
                    second(j - 2, expert[j - 2])
                if j + 2 < ALL:
                    transpose_x(j + 2)
                if j == AFTER["project"]:
                    project(3)
                if j == AFTER["z2T_2"]:
                    transpose_z2(2)
                if j == AFTER["logits_2"]:
                    logits(2)
                if j == AFTER["z2T_3"]:
                    transpose_z2(3)
                if j == AFTER["logits_3"]:
                    logits(3)
                if j == AFTER["ranks"]:
                    ranks(1)
                if j == AFTER["slot_list"]:
                    slot_list(1)


def kernel(**inputs):
    import concourse.bacc as _bacc
    from concourse.bass_utils import run_bass_kernel_spmd as _run

    def rows(name, *shape):
        return np.ascontiguousarray(np.asarray(inputs[name]).reshape(shape))

    def turned(name):
        return np.ascontiguousarray(np.asarray(inputs[name]).T)

    const, place = constants()
    g = [np.asarray(inputs[n]).reshape(1, 1) for n in ("g_xattn", "g_ffn")]
    arrays = {
        "x": rows("x", TOK, D),
        "ctx_t": np.ascontiguousarray(np.asarray(inputs["ctx_1024"]).reshape(BATCH * KV, D).T),
        "wq_t": turned("L0_xattn_Wq"), "wk_t": turned("L0_xattn_Wk"),
        "wv_t": turned("L0_xattn_Wv"), "wo_t": turned("L0_xattn_Wo"),
        "bcol": np.ascontiguousarray(np.concatenate(
            [np.asarray(inputs[f"L0_xattn_b{n}"]).reshape(2, P) for n in "qkv"]).T),
        "bo": rows("L0_xattn_bo", 1, D),
        "gates": np.ascontiguousarray(np.tile(np.concatenate(g, 1), (P, 1))),
        "router": rows("L0_ffn_router_w", D, E),
        "w_in": rows("L0_ffn_w_in", E, D, D), "w_out": rows("L0_ffn_w_out", E, D, D),
        "b_in": rows("L0_ffn_b_in", 1, E * D), "b_out": rows("L0_ffn_b_out", 1, E * D),
        "const": const,
    }
    nc = _bacc.Bacc("TRN2", target_bir_lowering=False, num_devices=1)
    aps = {n: nc.dram_tensor(f"in_{n}", v.shape, mybir.dt.from_np(v.dtype), kind="ExternalInput").ap()
           for n, v in arrays.items()}
    aps["out"] = nc.dram_tensor("out_0", (TOK, D), F32, kind="ExternalOutput").ap()
    build(nc, aps, place)
    r = _run(nc, [{f"in_{n}": v for n, v in arrays.items()}], core_ids=[0])
    return r.results[0]["out_0"].reshape(BATCH, SEQ, D)
```
